# Optimizing a Trainium2 kernel written in Bass

```python
import numpy as np
import jax
import jax.numpy as jnp

def _softmax(x, axis=-1):
    return jax.nn.softmax(x, axis=axis)

def _gelu(x):
    return jax.nn.gelu(x, approximate=True)

def _silu(x):
    return jax.nn.silu(x)

def _sigmoid(x):
    return jax.nn.sigmoid(x)

def _layernorm(x, axis=-1, eps=1e-05):
    m = jnp.mean(x, axis=axis, keepdims=True)
    v = jnp.var(x, axis=axis, keepdims=True)
    return (x - m) / jnp.sqrt(v + eps)

def _scatter_add(tgt, idx, src, axis=0):
    return tgt.at[idx].add(src)

def _segment_sum(src, seg, n):
    return jax.ops.segment_sum(src, seg, n)
kernel_name = 'mk_adj_preln_d2_adj_r2_941539'

def setup_inputs(seed: int=0):
    np.random.seed(seed)
    _w = jnp.asarray

    def _rec_inputs():
        import jax
        import jax.numpy as jnp
        _gk = jax.random.key(seed)
        x = 0.0001732 + 1 * jax.random.normal(jax.random.fold_in(_gk, 1), (5120, 64), jnp.float32)
        _w = (1.0 + jnp.arange(5120, dtype=jnp.float32)) ** (-0.5)
        _w = _w / _w.mean()
        _pij = jnp.clip(0.00078125 * _w[:, None] * _w[None, :], 0.0, 1.0)
        _a = jax.random.uniform(jax.random.fold_in(_gk, 2), (5120, 5120)) < _pij
        _af = _a.astype(jnp.float32)
        _af = _af * jax.random.uniform(jax.random.fold_in(_gk, 3), (5120, 5120), jnp.float32, 0.05, 0.02)
        adj = _af
        return (x, adj)
    x, adj = _rec_inputs()

    def _L0_gnn_setup():
        import jax, jax.numpy as jnp
        import numpy as np
        N_USERS = 2048
        N_ITEMS = 3072
        EMB = 64
        LN_EPS = 1e-05
        key = jax.random.key(seed)
        ks = jax.random.split(key, 10)
        N = N_USERS + N_ITEMS
        ego = jax.random.normal(ks[0], (N, EMB), jnp.float32)
        adj = (jax.random.uniform(ks[1], (N, N), jnp.float32) < 0.01).astype(jnp.float32) * 0.02
        xav = float(np.sqrt(6.0 / (EMB + EMB)))
        W_u = jax.random.uniform(ks[2], (EMB, EMB), jnp.float32, -xav, xav)
        W_i = jax.random.uniform(ks[3], (EMB, EMB), jnp.float32, -xav, xav)
        diag_u = jax.random.uniform(ks[4], (N_USERS,), jnp.float32, 0.99, 1.01)
        diag_i = jax.random.uniform(ks[5], (N_ITEMS,), jnp.float32, 0.99, 1.01)
        par_u = jax.random.uniform(ks[6], (2,), jnp.float32, 0.0, 0.99)
        par_i = jax.random.uniform(ks[7], (2,), jnp.float32, 0.0, 0.99)
        ln_gamma = jnp.ones((EMB,), jnp.float32)
        ln_beta = jnp.zeros((EMB,), jnp.float32)
        return {'ego_embeddings': ego, 'adj': adj, 'W_u': W_u, 'diag_u': diag_u, 'par_u': par_u, 'W_i': W_i, 'diag_i': diag_i, 'par_i': par_i, 'ln_gamma': ln_gamma, 'ln_beta': ln_beta}
    _L0_gnn_all = _L0_gnn_setup()
    _L0_gnn_in = {k: v for k, v in _L0_gnn_all.items() if k in ('W_u', 'diag_u', 'par_u', 'W_i', 'diag_i', 'par_i', 'ln_gamma', 'ln_beta')}
    del _L0_gnn_all

    def _L1_gnn_setup():
        import jax, jax.numpy as jnp
        import numpy as np
        N, D = (6144, 64)

        def _ggc(x, adj, W, wih, whh, bih, bhh):
            m = adj @ (x @ W)
            gi = m @ wih.T + bih
            gh = x @ whh.T + bhh
            i_r, i_z, i_n = jnp.split(gi, 3, axis=-1)
            h_r, h_z, h_n = jnp.split(gh, 3, axis=-1)
            r = jax.nn.sigmoid(i_r + h_r)
            z = jax.nn.sigmoid(i_z + h_z)
            n = jnp.tanh(i_n + r * h_n)
            return (1.0 - z) * n + z * x
        key = jax.random.key(seed)
        ks = jax.random.split(key, 8)
        s = 1.0 / np.sqrt(D)
        return {'x': jax.random.normal(ks[0], (N, D), jnp.float32), 'adj': jax.random.uniform(ks[1], (N, N), jnp.float32), 'W1': jax.random.normal(ks[2], (D, D), jnp.float32) * s, 'wih1': jax.random.normal(ks[3], (3 * D, D), jnp.float32) * s, 'whh1': jax.random.normal(ks[4], (3 * D, D), jnp.float32) * s, 'bih1': jnp.zeros((3 * D,), jnp.float32), 'bhh1': jnp.zeros((3 * D,), jnp.float32), 'W2': jax.random.normal(ks[5], (D, D), jnp.float32) * s, 'wih2': jax.random.normal(ks[6], (3 * D, D), jnp.float32) * s, 'whh2': jax.random.normal(ks[7], (3 * D, D), jnp.float32) * s, 'bih2': jnp.zeros((3 * D,), jnp.float32), 'bhh2': jnp.zeros((3 * D,), jnp.float32)}
    _L1_gnn_all = _L1_gnn_setup()
    _L1_gnn_in = {k: v for k, v in _L1_gnn_all.items() if k in ('W1', 'wih1', 'whh1', 'bih1', 'bhh1', 'W2', 'wih2', 'whh2', 'bih2', 'bhh2')}
    del _L1_gnn_all
    return {'x': x, 'adj': adj, 'L0_gnn_W_u': _L0_gnn_in['W_u'], 'L0_gnn_diag_u': _L0_gnn_in['diag_u'], 'L0_gnn_par_u': _L0_gnn_in['par_u'], 'L0_gnn_W_i': _L0_gnn_in['W_i'], 'L0_gnn_diag_i': _L0_gnn_in['diag_i'], 'L0_gnn_par_i': _L0_gnn_in['par_i'], 'L0_gnn_ln_gamma': _L0_gnn_in['ln_gamma'], 'L0_gnn_ln_beta': _L0_gnn_in['ln_beta'], 'L1_gnn_W1': _L1_gnn_in['W1'], 'L1_gnn_wih1': _L1_gnn_in['wih1'], 'L1_gnn_whh1': _L1_gnn_in['whh1'], 'L1_gnn_bih1': _L1_gnn_in['bih1'], 'L1_gnn_bhh1': _L1_gnn_in['bhh1'], 'L1_gnn_W2': _L1_gnn_in['W2'], 'L1_gnn_wih2': _L1_gnn_in['wih2'], 'L1_gnn_whh2': _L1_gnn_in['whh2'], 'L1_gnn_bih2': _L1_gnn_in['bih2'], 'L1_gnn_bhh2': _L1_gnn_in['bhh2']}

def reference(x, adj, L0_gnn_W_u, L0_gnn_diag_u, L0_gnn_par_u, L0_gnn_W_i, L0_gnn_diag_i, L0_gnn_par_i, L0_gnn_ln_gamma, L0_gnn_ln_beta, L1_gnn_W1, L1_gnn_wih1, L1_gnn_whh1, L1_gnn_bih1, L1_gnn_bhh1, L1_gnn_W2, L1_gnn_wih2, L1_gnn_whh2, L1_gnn_bih2, L1_gnn_bhh2):
    import jax
    import jax.numpy as jnp

    def _L0_gnn_ref(ego_embeddings, adj, W_u, diag_u, par_u, W_i, diag_i, par_i, ln_gamma, ln_beta):
        import jax, jax.numpy as jnp
        import numpy as np
        N_USERS = 2048
        N_ITEMS = 3072
        EMB = 64
        LN_EPS = 1e-05
        nu = diag_u.shape[0]
        res = ego_embeddings
        ego_u = ego_embeddings[:nu]
        ego_i = ego_embeddings[nu:]
        u = par_u[0] * par_u[1] * (diag_u[:, None] * ego_u @ W_u) + ego_u
        i = par_i[0] * par_i[1] * (diag_i[:, None] * ego_i @ W_i) + ego_i
        e = jnp.concatenate([u, i], axis=0)
        h = adj @ (adj.T @ e)
        mu = jnp.mean(h, axis=-1, keepdims=True)
        var = jnp.var(h, axis=-1, keepdims=True)
        out = (h - mu) * jax.lax.rsqrt(var + LN_EPS) * ln_gamma + ln_beta + res
        return out

    def _L1_gnn_ref(x, adj, W1, wih1, whh1, bih1, bhh1, W2, wih2, whh2, bih2, bhh2):
        import jax, jax.numpy as jnp
        import numpy as np
        N, D = (6144, 64)

        def _ggc(x, adj, W, wih, whh, bih, bhh):
            m = adj @ (x @ W)
            gi = m @ wih.T + bih
            gh = x @ whh.T + bhh
            i_r, i_z, i_n = jnp.split(gi, 3, axis=-1)
            h_r, h_z, h_n = jnp.split(gh, 3, axis=-1)
            r = jax.nn.sigmoid(i_r + h_r)
            z = jax.nn.sigmoid(i_z + h_z)
            n = jnp.tanh(i_n + r * h_n)
            return (1.0 - z) * n + z * x
        h = jax.nn.relu(_ggc(x, adj, W1, wih1, whh1, bih1, bhh1))
        return jax.nn.relu(_ggc(h, adj, W2, wih2, whh2, bih2, bhh2))
    h = jnp.maximum(_layernorm(x, axis=-1), 0.0)
    x = x + _L0_gnn_ref(h, adj, L0_gnn_W_u, L0_gnn_diag_u, L0_gnn_par_u, L0_gnn_W_i, L0_gnn_diag_i, L0_gnn_par_i, L0_gnn_ln_gamma, L0_gnn_ln_beta)
    h = jnp.maximum(_layernorm(x, axis=-1), 0.0)
    x = x + _L1_gnn_ref(h, adj, L1_gnn_W1, L1_gnn_wih1, L1_gnn_whh1, L1_gnn_bih1, L1_gnn_bhh1, L1_gnn_W2, L1_gnn_wih2, L1_gnn_whh2, L1_gnn_bih2, L1_gnn_bhh2)
    return x

_drawn_inputs = setup_inputs


def setup_inputs(seed=0):
    import zlib

    import numpy as np

    out = dict(_drawn_inputs(seed))
    spreads = {'L0_gnn_ln_gamma': (1.0, 0.2),
     'L0_gnn_ln_beta': (0.0, 0.1),
     'L1_gnn_bih1': (0.0, 0.8),
     'L1_gnn_bhh1': (0.0, 0.8),
     'L1_gnn_bih2': (0.0, 0.433),
     'L1_gnn_bhh2': (0.0, 0.8)}
    factors = {'L0_gnn_diag_u': 8.0,
     'L0_gnn_W_i': 3.029,
     'L0_gnn_diag_i': 8.0,
     'L1_gnn_W1': 4.684,
     'L1_gnn_wih1': 4.384,
     'L1_gnn_W2': 3.708,
     'L1_gnn_wih2': 3.712}
    for name, (base, spread) in spreads.items():
        noise = np.random.default_rng([zlib.crc32(name.encode()), seed]).standard_normal(out[name].shape)
        drawn = base * np.exp(spread * noise) if base else spread * noise
        out[name] = jnp.asarray(drawn.astype(out[name].dtype))
    for name, factor in factors.items():
        out[name] = (out[name] * factor).astype(out[name].dtype)
    return out
```

```python
from contextlib import ExitStack

import concourse.bass as bass
from concourse import mybir

F32 = mybir.dt.float32
ALU = mybir.AluOpType
ACT = mybir.ActivationFunctionType
AX = mybir.AxisListType

P = 128
D = 64
N = 5120
G = N // P
CACHED = 4
BLK = 512
GB = BLK // P
NR = N // BLK
NK = (N - CACHED * P) // BLK
LN_EPS = 1e-5
USER_GROUPS = 16
PAIRS = 5
NSTAGE = 4
NTURN = 3


def plan_sweeps():
    steps, chunks = [], []
    for t in range(2 * NR):
        R = t % NR
        if t < NR:
            ks = [k for k in range(NK) if k != R - 1]
            items = ks + ["cached"] + ([R - 1] if R > 0 else [])
        else:
            items = list(range(R, NK)) + ["cached"]
        gates_at = 0
        rows_at = max(0, min(4, len(items) - 2))
        for i, item in enumerate(items):
            if item == "cached":
                steps.append(("cached", t, R))
            else:
                steps.append(("chunk", len(chunks), t, R, item, i == 0))
                chunks.append((R, item))
            if t > 0 and i == gates_at:
                steps.append(("gates", t - 1))
            if t > 0 and i == rows_at:
                steps.append(("rows", t - 1))
                if 1 < t <= NR:
                    steps.append(("second", t - 1))
    steps += [("gates", 2 * NR - 1), ("rows", 2 * NR - 1)]
    return steps, chunks


def skewed(stages, counts):
    order = [(kind, stage, i - lag) for i in range(PAIRS + max(s[2] for s in stages))
             for kind, stage, lag in stages if 0 <= i - lag < PAIRS]
    at = {}
    for engine, (start, per) in counts.items():
        n = start
        for step in order:
            if step[:2] in per:
                n += per[step[:2]]
                at[(engine,) + step] = n
        at[engine] = n
    return order, at

DVE_SETUP = 7
PE_SETUP = 2

SETUP, setup_at = skewed(
    [("norm", "a", 0), ("norm", "b", 1), ("norm", "c", 2), ("turn", "", 2), ("keep", "", 2), ("prod", "", 3),
     ("e", "", 3)],
    {"dve": (DVE_SETUP, {("norm", "a"): 3, ("norm", "b"): 1, ("norm", "c"): 2, ("e", ""): 2}),
     "act": (0, {("norm", "a"): 1, ("norm", "b"): 1, ("norm", "c"): 1, ("keep", ""): 1}),
     "pe": (PE_SETUP, {("turn", ""): 1, ("prod", ""): 1})})
MIDDLE, mid_at = skewed(
    [("hrows", "", 0), ("norm1", "a", 0), ("norm1", "b", 1), ("norm1", "c", 2), ("norm2", "a", 3), ("norm2", "b", 4),
     ("norm2", "c", 5), ("turn", "", 5), ("keep", "", 5), ("y", "", 6), ("keep_y", "", 6)],
    {"dve": (0, {("norm1", "a"): 3, ("norm1", "b"): 1, ("norm1", "c"): 4, ("norm2", "a"): 3, ("norm2", "b"): 1,
                 ("norm2", "c"): 2, ("keep_y", ""): 1}),
     "act": (PAIRS, {("norm1", "a"): 1, ("norm1", "b"): 1, ("norm2", "a"): 1, ("norm2", "b"): 1,
                     ("norm2", "c"): 1, ("keep", ""): 4}),
     "pe": (0, {("hrows", ""): 1, ("turn", ""): 1, ("y", ""): 1})})


class Count:

    def __init__(self, sem):
        self.sem, self.n = sem, 0

    def up(self, instruction, by=1):
        self.n += by
        instruction.then_inc(self.sem, by)
        return self.n


def bass_two_layer_gnn(nc, x, adj, W_u, diag_u, par_u, W_i, diag_i, par_i, gamma, beta,
                       W1, wih1, whh1, bih1, bhh1, W2, wih2, whh2, bih2, bhh2, out):
    steps, chunks = plan_sweeps()
    POOL_X = 3 * PAIRS
    with ExitStack() as ctx:
        def sb(name, shape):
            return ctx.enter_context(nc.sbuf_tensor(name, shape, F32))

        def sem(name):
            return ctx.enter_context(nc.semaphore(name))

        at = sb("at", [P, CACHED, N])
        arena = sb("arena", [P, 14336])
        xs = sb("xs", [P, G, D])
        es = sb("es", [P, G, D])
        y1 = sb("y1", [P, G, D])
        hs = sb("hs", [P, N])
        work = sb("work", [P, 5, BLK])
        outs = sb("outs", [P, 2, GB * D])
        ident = sb("ident", [P, P])
        twice = sb("twice", [P, D])
        w_ui = sb("w_ui", [D, 2, D])
        w_rz = sb("w_rz", [P, 2, P])
        w_n = sb("w_n", [P, 2, P])
        w_12 = sb("w_12", [P, 2, D])
        gam = sb("gam", [P, D])
        bet = sb("bet", [P, D])
        b_ih = sb("b_ih", [P, 2, 2])
        b_hh = sb("b_hh", [P, 2, 2])
        b_rz = sb("b_rz", [P, 2])
        par = sb("par", [P, 2, 2])
        parp = sb("parp", [P, 2])
        dT = sb("dT", [G, P])
        coef = sb("coef", [P, G])
        eps = sb("eps", [P, 1])
        stat = sb("stat", [P, PAIRS, 4, 8])
        zT = sb("zT", [P, P])
        zs = sb("zs", [P, 2, D])

        nat = arena[:, 0:2 * G * P].rearrange("p (s g c) -> p s g c", s=2, g=G)
        incoming = arena[:, 0:NSTAGE * 2048].rearrange("p (s f) -> p s f", s=NSTAGE)
        turned = arena[:, NSTAGE * 2048:(NSTAGE + NTURN) * 2048].rearrange("p (s j i) -> p s j i", s=NTURN, j=GB)
        raw = y1[:, 32:40, :].rearrange("p (w h) d -> p w h d", w=4)
        h0T = y1[:, 0:32, :].rearrange("p (s g) d -> p s (g d)", s=2)
        hT = es[:].rearrange("p g d -> p (g d)")
        y2 = es
        scratch = [hs[:, :].rearrange("p (s f) -> p s f", s=10),
                   arena[:, NSTAGE * 2048:NSTAGE * 2048 + 5120].rearrange("p (s f) -> p s f", s=10)]

        ps = ctx.enter_context(nc.psum_tensor("ps", [P, 8, BLK], F32))
        Z_BANK, TP_BANK = 5, 6

        s_x = sem("x_loaded")
        s_w = sem("weights_loaded")
        s_idg = sem("identity_on_pool")
        s_id = sem("identity_ready")
        s_dve = sem("dve_steps")
        s_dve2 = sem("dve_mid_steps")
        s_act = sem("act_steps")
        s_act2 = sem("act_mid_steps")
        s_pe = sem("pe_setup_steps")
        s_pe2 = sem("pe_mid_steps")
        s_pool = sem("pool_steps")
        s_nat = [sem(f"block_loaded_{i}") for i in range(2)]
        s_tp = sem("transposes_done")
        s_ta = sem("transposes_kept_by_act")
        s_tv = sem("transposes_kept_by_dve")
        s_zT = sem("z_transposed_done")
        s_zc = sem("z_transposed_copied")
        s_zn = sem("z_rows_done")
        s_z = sem("z_ready")
        s_p2 = sem("block_product_done")
        s_stage = [sem(f"chunk_loaded_{i}") for i in range(NSTAGE)]
        s_turn = sem("chunk_transposed")
        s_used = sem("chunk_used")
        s_m1 = sem("product_done")
        s_mt = sem("upper_half_moved")
        s_m = sem("product_kept")
        s_g = sem("gates_done")
        s_rz = sem("sigmoid_done")
        s_u = sem("tanh_input_ready")
        s_n = sem("tanh_done")
        s_hv = sem("new_state_ready")
        s_h = sem("new_state_kept")
        s_r = sem("rows_done")
        s_y = sem("rows_kept")
        s_m2t = sem("second_upper_half_moved")
        s_m2k = sem("second_product_kept")
        s_gd = sem("gate_steps")
        s_out = [sem(f"stored_{i}") for i in range(2)]

        weight_loads = [
            (dT[0:USER_GROUPS, :], diag_u.rearrange("(g p) -> g p", p=P)),
            (dT[USER_GROUPS:G, :], diag_i.rearrange("(g p) -> g p", p=P)),
            (par[:, 0, :], par_u.partition_broadcast(P)),
            (par[:, 1, :], par_i.partition_broadcast(P)),
            (w_ui[:, 0, :], W_u), (w_ui[:, 1, :], W_i),
            (gam[:], gamma.partition_broadcast(P)), (bet[:], beta.partition_broadcast(P)),
            (w_12[D:P, 0, :], W1), (w_12[D:P, 1, :], W2),
        ]
        for w, m in enumerate((wih1, whh1, wih2, whh2)):
            weight_loads += [(raw[:, w, 0, :], m[0:P, :]), (raw[0:D, w, 1, :], m[P:3 * D, :])]
        for l, (bi, bh) in enumerate(((bih1, bhh1), (bih2, bhh2))):
            weight_loads += [
                (b_ih[:, l, 0:1], bi[0:P].rearrange("(p o) -> p o", o=1)),
                (b_hh[:, l, 0:1], bh[0:P].rearrange("(p o) -> p o", o=1)),
                (b_ih[D:P, l, 1:2], bi[P:3 * D].rearrange("(p o) -> p o", o=1)),
                (b_hh[0:D, l, 1:2], bh[P:3 * D].rearrange("(p o) -> p o", o=1)),
            ]
        WEIGHTS_IN = 16 * len(weight_loads)

        def pair(buf, c):
            return buf[:].rearrange("p (h g) d -> p h g d", h=2)[:, :, 4 * c:4 * c + 4, :]

        def eight(ap):
            return ap.rearrange("p (h g d) -> p h g d", h=2, g=4)

        def spread(col):
            return col.rearrange("p (h g o) -> p h g o", h=2, o=1).broadcast_to([P, 2, 4, D])

        def spread3(col):
            return col.rearrange("p (g o) -> p g o", o=1).broadcast_to([P, 8, D])

        def rows_of(row):
            return row.rearrange("p (g d) -> p g d", g=1).broadcast_to([P, 8, D])

        def group_of(c, i):
            return 4 * c + i if i < 4 else 20 + 4 * c + i - 4

        def in_group_order(R, natural):
            if R * GB >= G - CACHED:
                return natural.rearrange("p (q j b) -> p q j b", q=4, b=32)
            return natural.rearrange("p (j q b) -> p q j b", q=4, b=32)

        def quarters(ap):
            return ap.rearrange("p (q j b) -> p q j b", q=4, b=32)

        last_of = {s[2 if s[0] == "chunk" else 1]: s for s in steps if s[0] in ("chunk", "cached")}

        block = ctx.enter_context(nc.Block())

        @block.sync
        def _(sp):
            sp.dma_start(xs[:], x.rearrange("(g p) d -> p g d", p=P)).then_inc(s_x, 16)

            def load_block(col, slot):
                sp.dma_start(nat[:, slot], adj[:, bass.ds(col, P)].rearrange("(g p) c -> p g c", p=P)
                             ).then_inc(s_nat[slot], 16)

            load_block(0, 0)
            load_block(P, 1)
            with sp.Fori(1, G // 2) as pr:
                for i in range(2):
                    sp.wait_ge(s_zT, pr * 2 + (i - 1))
                    load_block(pr * (2 * P) + i * P, i)

            sp.wait_ge(s_zT, G)
            for n, (R, k) in enumerate(chunks):
                slot = n % NSTAGE
                if n >= NSTAGE:
                    sp.wait_ge(s_turn, n - NSTAGE + 1)
                rows = adj[R * BLK:(R + 1) * BLK, :].rearrange("(i a) c -> a i c", a=32)
                for q in range(4):
                    sp.dma_start(incoming[32 * q:32 * q + 32, slot].rearrange("p (i c) -> p i c", c=P),
                                 rows[:, :, k * BLK + q * P:k * BLK + (q + 1) * P]).then_inc(s_stage[slot], 16)

        @block.gpsimd
        def _(pool):
            own = Count(s_idg)
            n = own.up(nc.gpsimd.memset(ident[:], 0.0))
            pool.wait_ge(s_idg, n)
            nc.gpsimd.affine_select(out=ident[:], in_=ident[:], compare_op=ALU.not_equal, fill=1.0, base=0,
                                    pattern=[[-1, P]], channel_multiplier=1).then_inc(s_id, 1)
            pool.wait_ge(s_w, WEIGHTS_IN)
            done = Count(s_pool)
            for c in range(PAIRS):
                pool.wait_ge(s_act, setup_at["act", "norm", "c", c])
                xv = pair(xs, c)
                n = done.up(nc.gpsimd.tensor_tensor(xv, xv, eight(scratch[0][:, 5 + c, :]), ALU.add))
                pool.wait_ge(s_pool, n)
                for h in range(2):
                    v = xs[:, 20 * h + 4 * c:20 * h + 4 * c + 4, :]
                    done.up(nc.gpsimd.tensor_tensor(
                        v, v, bet[:].rearrange("p (g d) -> p g d", g=1).broadcast_to([P, 4, D]), ALU.add))

        @block.scalar
        def _(act):
            for dst, src in weight_loads:
                act.dma_start(dst, src).then_inc(s_w, 16)

            def norm_step(stage, c, centred, s_d, s_a, sc):
                act.wait_ge(s_d, centred)
                if stage == "a":
                    nc.scalar.activation(sc[:, 5 + c, :], sc[:, c, :], ACT.Square).then_inc(s_a, 1)
                elif stage == "b":
                    nc.scalar.activation(stat[:, c, 2, :], stat[:, c, 1, :], ACT.Sqrt, bias=eps[:], scale=1.0 / D
                                         ).then_inc(s_a, 1)
                else:
                    nc.scalar.activation(sc[:, 5 + c, :], sc[:, c, :], ACT.Relu).then_inc(s_a, 1)

            for kind, stage, c in SETUP:
                if kind == "norm":
                    norm_step(stage, c, setup_at["dve", "norm", stage, c], s_dve, s_act, scratch[0])
                elif kind == "keep":
                    act.wait_ge(s_pe, setup_at["pe", "turn", "", c])
                    if c >= 2:
                        act.wait_ge(s_pe, setup_at["pe", "prod", "", c - 2])
                    nc.scalar.activation(h0T[0:D, c % 2, :].rearrange("p (b f) -> p b f", b=2),
                                         ps[0:D, 2 * (c % 2):2 * (c % 2) + 2, :], ACT.Copy).then_inc(s_act, 1)

            def keep_z(b, half):
                act.wait_ge(s_zn, b + 1)
                nc.scalar.activation(zs[:, half, :], ps[:, TP_BANK + 1, 0:D], ACT.Copy).then_inc(s_z, 1)

            def keep_transposes(b, slot, first, z_of=None):
                for s in range(0, 10, 2):
                    act.wait_ge(s_tp, b * 10 + (s + 1))
                    if s == 0 and not first:
                        act.wait_ge(s_p2, b - 1)
                    nc.scalar.activation(at[:, slot, s * BLK:(s + 1) * BLK], ps[:, TP_BANK, :], ACT.Copy
                                         ).then_inc(s_ta, 1)
                    if s == 0 and z_of:
                        keep_z(*z_of)

            keep_transposes(0, 0, True)
            keep_transposes(1, 1, True, (0, 0))
            with act.Fori(2, G - CACHED, 2) as b:
                for i in range(2):
                    keep_transposes(b + i, i, False, (b + (i - 1), 1 - i))
            for b in range(G - CACHED, G):
                keep_transposes(b, b - (G - CACHED), False, (b - 1, (b - 1) % 2))
            keep_z(G - 1, (G - 1) % 2)

            act.wait_ge(s_p2, G)
            for c in range(PAIRS):
                nc.scalar.activation(hT[:, c * BLK:(c + 1) * BLK], ps[:, c, :], ACT.Copy).then_inc(s_act2, 1)
            for kind, stage, c in MIDDLE:
                if kind == "norm2" or (kind == "norm1" and stage != "c"):
                    norm_step(stage, c, mid_at["dve", kind, stage, c], s_dve2, s_act2, scratch[1])
                elif kind == "keep":
                    act.wait_ge(s_pe2, mid_at["pe", "turn", "", c])
                    for h in range(2):
                        nc.scalar.activation(hs[D:P, (h * 20 + 4 * c) * P:(h * 20 + 4 * c + 4) * P],
                                             ps[D:P, 4 + h, :], ACT.Copy).then_inc(s_act2, 1)
                        nc.scalar.activation(in_group_order(c + 5 * h, work[D:P, 2 * (c % 2) + h, :]),
                                             quarters(ps[D:P, 4 + h, :]), ACT.Copy).then_inc(s_act2, 1)

            for step in steps:
                if step[0] == "gates":
                    t = step[1]
                    l, R = t // NR, t % NR
                    cols = slice(R * BLK, (R + 1) * BLK)
                    act.wait_ge(s_m1, t + 1)
                    if t > 0:
                        act.wait_ge(s_m, t)
                    nc.scalar.activation(work[0:D, 0, :], ps[D:P, t % 2, :], ACT.Copy).then_inc(s_mt, 1)
                    act.wait_ge(s_g, t + 1)
                    if t > 0:
                        act.wait_ge(s_hv, t)
                    nc.scalar.activation(work[:, 1, :], ps[:, 4, :], ACT.Sigmoid, bias=b_rz[:, l:l + 1]
                                         ).then_inc(s_rz, 1)
                    act.wait_ge(s_u, t + 1)
                    nc.scalar.activation(work[D:P, 3, :], work[D:P, 2, :], ACT.Tanh, bias=b_ih[D:P, l, 1:2]
                                         ).then_inc(s_n, 1)
                    act.wait_ge(s_hv, t + 1)
                    if t < NR:
                        nc.scalar.activation(hs[D:P, cols], work[D:P, 2, :], ACT.Relu)
                        nc.scalar.activation(in_group_order(R, work[D:P, 0, :]), quarters(work[D:P, 2, :]), ACT.Relu
                                             ).then_inc(s_h, 1)
                    else:
                        nc.scalar.activation(hs[D:P, cols], work[D:P, 2, :], ACT.Relu).then_inc(s_h, 1)
                elif step[0] == "rows":
                    t = step[1]
                    R = t % NR
                    act.wait_ge(s_r, t + 1)
                    if t < NR:
                        nc.scalar.activation(y2[:, GB * R:GB * R + GB, :].rearrange("p g d -> p (g d)"),
                                             ps[:, 6, 0:GB * D], ACT.Copy).then_inc(s_y, 1)
                    else:
                        act.wait_ge(s_y, t + 1)
                        act.dma_start(out[R * BLK:(R + 1) * BLK, :].rearrange("(g p) d -> p g d", p=P),
                                      outs[:, R % 2, :].rearrange("p (g d) -> p g d", d=D)
                                      ).then_inc(s_out[R % 2], 16)
                elif step[0] == "second":
                    R = step[1]
                    act.wait_ge(s_used, last_of[R][1] + 1)
                    if R > 1:
                        act.wait_ge(s_m2k, R - 1)
                    nc.scalar.activation(work[0:D, 4, :], ps[D:P, 2 + R % 2, :], ACT.Copy).then_inc(s_m2t, 1)
            for i in range(2):
                act.wait_ge(s_out[i], 16 * (NR // 2))

        @block.vector
        def _(dve):
            own = Count(s_dve)
            own.up(nc.vector.memset(eps[:], LN_EPS))
            n = own.up(nc.vector.memset(w_n[:], 0.0))
            dve.wait_ge(s_w, WEIGHTS_IN)
            own.up(nc.vector.tensor_tensor(parp[:], par[:, :, 0], par[:, :, 1], ALU.mult))
            own.up(nc.vector.tensor_tensor(b_rz[:], b_ih[:, :, 0], b_hh[:, :, 0], ALU.add))
            dve.wait_ge(s_id, 1)
            n = own.up(nc.vector.tensor_tensor(twice[:], ident[:, 0:D], ident[:, D:P], ALU.add))
            dve.wait_ge(s_pe, 2)
            dve.wait_ge(s_dve, n)
            last = None
            for (g0, g1, w) in ((0, USER_GROUPS, 0), (USER_GROUPS, G, 1)):
                last = nc.vector.tensor_scalar(coef[:, g0:g1], ps[:, 7, g0:g1], parp[:, w:w + 1], None, ALU.mult)
            own.up(last)
            for l in range(2):
                nc.vector.tensor_copy(w_rz[:, l, :], ps[:, 4 + l, 0:P])
                nc.vector.tensor_copy(w_n[0:D, l, D:P], ps[0:D, 4 + l, P + D:2 * P])
                last = nc.vector.tensor_copy(w_n[D:P, l, 0:D], ps[D:P, 4 + l, P:P + D])
            own.up(last)
            assert own.n == DVE_SETUP

            def norm_step(cnt, stg, c, src, s_a, a_done, sc):
                st = stat[:, c]
                if stg == "a":
                    n = cnt.up(nc.vector.tensor_reduce(st[:, 0, :], src, AX.X, ALU.add))
                    dve.wait_ge(cnt.sem, n)
                    n = cnt.up(nc.vector.tensor_scalar(st[:, 0, :], st[:, 0, :], -1.0 / D, None, ALU.mult))
                    dve.wait_ge(cnt.sem, n)
                    if len(src.shape) == 4:
                        cnt.up(nc.vector.tensor_tensor(eight(sc[:, c, :]), src, spread(st[:, 0, :]), ALU.add))
                    else:
                        cnt.up(nc.vector.tensor_tensor(sc[:, c, :].rearrange("p (g d) -> p g d", d=D), src,
                                                       spread3(st[:, 0, :]), ALU.add))
                elif stg == "b":
                    dve.wait_ge(s_a, a_done)
                    cnt.up(nc.vector.tensor_reduce(st[:, 1, :], sc[:, 5 + c, :].rearrange("p (g d) -> p g d", d=D),
                                                   AX.X, ALU.add))
                else:
                    dve.wait_ge(s_a, a_done)
                    n = cnt.up(nc.vector.reciprocal(st[:, 3, :], st[:, 2, :]))
                    dve.wait_ge(cnt.sem, n)
                    v = sc[:, c, :].rearrange("p (g d) -> p g d", d=D)
                    cnt.up(nc.vector.tensor_tensor(v, v, spread3(st[:, 3, :]), ALU.mult))

            dve.wait_ge(s_x, 16)
            for kind, stage, c in SETUP:
                if kind == "norm":
                    before = {"a": None, "b": "a", "c": "b"}[stage]
                    norm_step(own, stage, c, pair(xs, c), s_act,
                              before and setup_at["act", "norm", before, c], scratch[0])
                elif kind == "e":
                    dve.wait_ge(s_pe, setup_at["pe", "prod", "", c])
                    for h in range(2):
                        g0 = 20 * h + 4 * c
                        last = nc.vector.tensor_tensor(
                            es[:, g0:g0 + 4, :],
                            ps[:, 4, h * 4 * D:(h + 1) * 4 * D].rearrange("p (g d) -> p g d", d=D),
                            coef[:, g0:g0 + 4].rearrange("p (g o) -> p g o", o=1).broadcast_to([P, 4, D]), ALU.mult)
                    n = own.up(last)
                    dve.wait_ge(s_dve, n)
                    own.up(nc.vector.tensor_tensor(pair(es, c), pair(es, c), eight(scratch[0][:, 5 + c, :]), ALU.add))
            assert own.n == setup_at["dve"]

            def keep_transposes(b, slot, first):
                for s in range(1, 10, 2):
                    dve.wait_ge(s_tp, b * 10 + (s + 1))
                    if s == 1 and not first:
                        dve.wait_ge(s_p2, b - 1)
                    nc.vector.tensor_copy(at[:, slot, s * BLK:(s + 1) * BLK], ps[:, TP_BANK + 1, :]
                                          ).then_inc(s_tv, 1)

            def keep_zT(b):
                dve.wait_ge(s_zT, b + 1)
                nc.vector.tensor_copy(zT[:], ps[:, Z_BANK, 0:P]).then_inc(s_zc, 1)

            keep_transposes(0, 0, True)
            keep_zT(0)
            keep_transposes(1, 1, True)
            with dve.Fori(2, G - CACHED, 2) as b:
                for i in range(2):
                    keep_zT(b + (i - 1))
                    keep_transposes(b + i, i, False)
            for b in range(G - CACHED, G):
                keep_zT(b - 1)
                keep_transposes(b, b - (G - CACHED), False)
            keep_zT(G - 1)

            mid = Count(s_dve2)
            sc = scratch[1]
            for kind, stage, c in MIDDLE:
                if kind in ("norm1", "norm2"):
                    if stage == "a":
                        if kind == "norm1":
                            dve.wait_ge(s_pe2, mid_at["pe", "hrows", "", c])
                            src = ps[:, 6 + c % 2, :].rearrange("p (g h d) -> p h g d", h=2, d=D)
                        else:
                            dve.wait_ge(s_dve2, mid_at["dve", "norm1", "c", c])
                            src = pair(xs, c)
                        norm_step(mid, "a", c, src, None, None, sc)
                    else:
                        norm_step(mid, stage, c, None, s_act2,
                                  mid_at["act", kind, "a" if stage == "b" else "b", c], sc)
                    if kind == "norm1" and stage == "c":
                        dve.wait_ge(s_dve2, mid.n)
                        v = sc[:, c, :].rearrange("p (g d) -> p g d", d=D)
                        n = mid.up(nc.vector.tensor_tensor(v, v, rows_of(gam[:]), ALU.mult))
                        dve.wait_ge(s_dve2, n)
                        dve.wait_ge(s_pool, POOL_X)
                        mid.up(nc.vector.tensor_tensor(pair(xs, c), eight(sc[:, c, :]), pair(xs, c), ALU.add))
                elif kind == "keep_y":
                    dve.wait_ge(s_pe2, mid_at["pe", "y", "", c])
                    mid.up(nc.vector.tensor_copy(pair(y1, c), eight(ps[:, 3, :])))
            assert mid.n == mid_at["dve"]

            def turn_chunk(n):
                slot, to = n % NSTAGE, n % NTURN
                dve.wait_ge(s_stage[slot], 64 * (n // NSTAGE + 1))
                if n >= NTURN:
                    dve.wait_ge(s_used, n - NTURN + 1)
                nc.vector.transpose(turned[:, to].rearrange("p j (i a) -> p i j a", a=32),
                                    incoming[:, slot].rearrange("p (i j b) -> p i j b", j=GB, b=32)
                                    ).then_inc(s_turn, 1)

            g = Count(s_gd)
            dve.wait_ge(s_pe2, mid_at["pe", "turn", "", PAIRS - 1])
            turn_chunk(0)
            turn_chunk(1)
            for step in steps:
                if step[0] == "chunk":
                    if step[1] + 2 < len(chunks):
                        turn_chunk(step[1] + 2)
                elif step[0] == "gates":
                    t = step[1]
                    l, R = t // NR, t % NR
                    cols = slice(R * BLK, (R + 1) * BLK)
                    dve.wait_ge(s_mt, t + 1)
                    if t > NR:
                        n = g.up(nc.vector.tensor_tensor(work[0:D, 0, :], work[0:D, 0, :], hs[0:D, cols], ALU.add))
                        dve.wait_ge(s_gd, n)
                    nc.vector.tensor_tensor(hs[0:D, cols], ps[0:D, t % 2, :], work[0:D, 0, :], ALU.add
                                            ).then_inc(s_m, 1)
                    dve.wait_ge(s_rz, t + 1)
                    n = g.up(nc.vector.scalar_tensor_tensor(out=work[D:P, 2, :], in0=ps[0:D, 5, :],
                                                            scalar=b_hh[0:D, l, 1:2], in1=work[0:D, 1, :],
                                                            op0=ALU.add, op1=ALU.mult))
                    dve.wait_ge(s_gd, n)
                    nc.vector.tensor_tensor(work[D:P, 2, :], ps[D:P, 5, :], work[D:P, 2, :], ALU.add
                                            ).then_inc(s_u, 1)
                    dve.wait_ge(s_n, t + 1)
                    n = g.up(nc.vector.tensor_tensor(work[D:P, 2, :], hs[D:P, cols], work[D:P, 3, :], ALU.subtract))
                    dve.wait_ge(s_gd, n)
                    n = g.up(nc.vector.tensor_tensor(work[D:P, 2, :], work[D:P, 2, :], work[D:P, 1, :], ALU.mult))
                    dve.wait_ge(s_gd, n)
                    nc.vector.tensor_tensor(work[D:P, 2, :], work[D:P, 2, :], work[D:P, 3, :], ALU.add
                                            ).then_inc(s_hv, 1)
                elif step[0] == "rows" and step[1] >= NR:
                    t = step[1]
                    R = t % NR
                    dve.wait_ge(s_r, t + 1)
                    if R >= 2:
                        dve.wait_ge(s_out[R % 2], 16 * (R // 2))
                    nc.vector.tensor_tensor(outs[:, R % 2, :], ps[:, 6, 0:GB * D],
                                            xs[:, GB * R:GB * R + GB, :].rearrange("p g d -> p (g d)"), ALU.add
                                            ).then_inc(s_y, 1)
                elif step[0] == "second":
                    R = step[1]
                    dve.wait_ge(s_m2t, R)
                    nc.vector.tensor_tensor(hs[0:D, R * BLK:(R + 1) * BLK], ps[0:D, 2 + R % 2, :], work[0:D, 4, :],
                                            ALU.add).then_inc(s_m2k, 1)

        @block.tensor
        def _(pe):
            mm = nc.tensor.matmul
            pe.wait_ge(s_w, WEIGHTS_IN)
            pe.wait_ge(s_id, 1)
            mm(ps[:, 7, 0:G], dT[:, :], ident[0:G, 0:G], start=True, stop=True).then_inc(s_pe, 1)
            for l in range(2):
                ih, hh = raw[:, 2 * l], raw[:, 2 * l + 1]
                mm(ps[0:D, 4 + l, 0:P], ih[:, 0, :], ident[:, :], start=True, stop=True)
                mm(ps[D:P, 4 + l, 0:P], hh[:, 0, :], ident[:, :], start=True, stop=True)
                mm(ps[0:D, 4 + l, P + D:2 * P], ih[0:D, 1, :], ident[0:D, 0:D], start=True, stop=True)
                last = mm(ps[D:P, 4 + l, P:P + D], hh[0:D, 1, :], ident[0:D, 0:D], start=True, stop=True)
            last.then_inc(s_pe, 1)
            for kind, _, c in SETUP:
                if kind == "turn":
                    pe.wait_ge(s_act, setup_at["act", "norm", "c", c])
                    if c >= 2:
                        pe.wait_ge(s_act, setup_at["act", "keep", "", c - 2])
                    for i in range(8):
                        last = mm(ps[0:D, 2 * (c % 2) + i // 4, (i % 4) * P:(i % 4 + 1) * P],
                                  scratch[0][:, 5 + c, i * D:(i + 1) * D], ident[:, :], start=True, stop=True)
                    last.then_inc(s_pe, 1)
                elif kind == "prod":
                    pe.wait_ge(s_act, setup_at["act", "keep", "", c])
                    pe.wait_ge(s_dve, setup_at["dve", "e", "", c - 1] if c else DVE_SETUP)
                    for i in range(8):
                        last = mm(ps[:, 4, i * D:(i + 1) * D], h0T[0:D, c % 2, i * P:(i + 1) * P],
                                  w_ui[:, 0 if group_of(c, i) < USER_GROUPS else 1, :], start=True, stop=True)
                    last.then_inc(s_pe, 1)

            def h_products(b, slot, half, first, last_block, which):
                done = None
                for m in which:
                    h, bank = m % 2, m // 2
                    done = mm(ps[D * h:D * h + D, bank, :], zs[:, half, :],
                              at[:, slot, (h * 5 + bank) * BLK:(h * 5 + bank + 1) * BLK],
                              start=first, stop=last_block, skip_group_check=True)
                return done

            def z_rows(b):
                pe.wait_ge(s_zc, b + 1)
                mm(ps[:, TP_BANK + 1, 0:D], zT[:], twice[:], start=True, stop=True, skip_group_check=True
                   ).then_inc(s_zn, 1)

            def iteration(b, slot, buf, nat_wait, prev):
                for s in range(10):
                    if s == 0:
                        pe.wait_ge(s_nat[buf], nat_wait)
                    if s % 2 == 0:
                        pe.wait_ge(s_ta, b * 5 + s // 2)
                    else:
                        pe.wait_ge(s_tv, b * 5 + s // 2)
                        if s == 1:
                            pe.wait_ge(s_z, b)
                    for i in range(4):
                        last = nc.tensor.transpose(ps[:, TP_BANK + s % 2, i * P:(i + 1) * P],
                                                   nat[:, buf, 4 * s + i, :], ident[:])
                    last.then_inc(s_tp, 1)
                    if s == 0:
                        pe.wait_ge(s_tv, b * 5)
                        z_rows(b - 1)
                    for i in range(4):
                        g = 4 * s + i
                        last = mm(ps[D * (g % 2):D * (g % 2) + D, Z_BANK, 0:P], es[:, g, :], nat[:, buf, g, :],
                                  start=g < 2, stop=g >= G - 2, skip_group_check=True)
                    if s == 9:
                        last.then_inc(s_zT, 1)
                    if s % 2 == 1:
                        done = h_products(b - 1, prev[0], prev[1], prev[2], False, (s - 1, s))
                        if s == 9:
                            done.then_inc(s_p2, 1)

            pe.wait_ge(s_dve, setup_at["dve"])
            for s in range(10):
                if s == 0:
                    pe.wait_ge(s_nat[0], 16)
                if s >= 2:
                    if s % 2 == 0:
                        pe.wait_ge(s_ta, s // 2)
                    else:
                        pe.wait_ge(s_tv, s // 2)
                for i in range(4):
                    last = nc.tensor.transpose(ps[:, TP_BANK + s % 2, i * P:(i + 1) * P], nat[:, 0, 4 * s + i, :],
                                               ident[:])
                last.then_inc(s_tp, 1)
                for i in range(4):
                    g = 4 * s + i
                    last = mm(ps[D * (g % 2):D * (g % 2) + D, Z_BANK, 0:P], es[:, g, :], nat[:, 0, g, :],
                              start=g < 2, stop=g >= G - 2, skip_group_check=True)
            last.then_inc(s_zT, 1)
            iteration(1, 1, 1, 16, prev=(0, 0, True))
            with pe.Fori(2, G - CACHED, 2) as b:
                for i in range(2):
                    iteration(b + i, i, i, b * 8 + 16, prev=(1 - i, 1 - i, False))
            for b in range(G - CACHED, G):
                slot = b - (G - CACHED)
                iteration(b, slot, b % 2, 16 * (b // 2 + 1), prev=(1 if slot == 0 else slot - 1, (b - 1) % 2, False))
            pe.wait_ge(s_ta, 5 * G)
            pe.wait_ge(s_tv, 5 * G)
            z_rows(G - 1)
            pe.wait_ge(s_z, G)
            h_products(G - 1, CACHED - 1, (G - 1) % 2, False, True, range(10)).then_inc(s_p2, 1)

            for kind, _, c in MIDDLE:
                if kind == "hrows":
                    pe.wait_ge(s_act2, c + 1)
                    if c >= 2:
                        pe.wait_ge(s_dve2, mid_at["dve", "norm1", "a", c - 2])
                    for i in range(GB):
                        last = mm(ps[:, 6 + c % 2, i * P:(i + 1) * P], hT[:, c * BLK + i * P:c * BLK + (i + 1) * P],
                                  ident[:, :], start=True, stop=True)
                    last.then_inc(s_pe2, 1)
                elif kind == "turn":
                    pe.wait_ge(s_act2, mid_at["act", "norm2", "c", c])
                    if c >= 1:
                        pe.wait_ge(s_act2, mid_at["act", "keep", "", c - 1])
                    else:
                        pe.wait_ge(s_act2, PAIRS)
                    for i in range(8):
                        last = mm(ps[D:P, 4 + i // 4, (i % 4) * P:(i % 4 + 1) * P],
                                  scratch[1][:, 5 + c, i * D:(i + 1) * D], ident[:, :], start=True, stop=True)
                    last.then_inc(s_pe2, 1)
                elif kind == "y":
                    pe.wait_ge(s_act2, mid_at["act", "keep", "", c])
                    if c >= 1:
                        pe.wait_ge(s_dve2, mid_at["dve", "keep_y", "", c - 1])
                    for i in range(8):
                        last = mm(ps[:, 3, i * D:(i + 1) * D], work[D:P, 2 * (c % 2) + i // 4, (i % 4) * P:(i % 4 + 1) * P], w_12[D:P, 0, :],
                                  start=True, stop=True)
                    last.then_inc(s_pe2, 1)

            for step in steps:
                if step[0] in ("chunk", "cached"):
                    if step[0] == "chunk":
                        _, n, t, R, k, start = step
                        pe.wait_ge(s_turn, n + 1)
                    else:
                        _, t, R = step
                        k, start = NK, t == 2 * NR - 1
                    if t == 0:
                        pe.wait_ge(s_dve2, mid_at["dve", "keep_y", "", k % PAIRS])
                    elif t >= NR:
                        pe.wait_ge(s_y, min(k, NR - 1) + 1)
                    if start and t >= 2:
                        pe.wait_ge(s_m, t - 1)
                    ys = y1 if t < NR else y2
                    second = t < NR and k < R and step[0] == "chunk"
                    if second:
                        pe.wait_ge(s_y, k + 1)
                        if k == 0 and R >= 3:
                            pe.wait_ge(s_m2k, R - 2)
                    ends = last_of[t] == step
                    for j in range(GB):
                        moving = (turned[:, n % NTURN, j, :] if step[0] == "chunk"
                                  else at[:, j, R * BLK:(R + 1) * BLK])
                        h = j % 2
                        last = mm(ps[D * h:D * h + D, t % 2, :], ys[:, GB * k + j, :], moving,
                                  start=start and j < 2, stop=ends and j >= 2, skip_group_check=True)
                    if ends:
                        last.then_inc(s_m1, 1)
                    if second:
                        for j in range(GB):
                            h = j % 2
                            last = mm(ps[D * h:D * h + D, 2 + R % 2, :], y2[:, GB * k + j, :],
                                      turned[:, n % NTURN, j, :], start=k == 0 and j < 2,
                                      stop=k == R - 1 and j >= 2, skip_group_check=True)
                    if step[0] == "chunk":
                        last.then_inc(s_used, 1)
                elif step[0] == "gates":
                    t = step[1]
                    l, R = t // NR, t % NR
                    pe.wait_ge(s_m, t + 1)
                    if t >= 1:
                        pe.wait_ge(s_u, t)
                    mm(ps[:, 4, :], w_rz[:, l, :], hs[:, R * BLK:(R + 1) * BLK], start=True, stop=True)
                    mm(ps[:, 5, :], w_n[:, l, :], hs[:, R * BLK:(R + 1) * BLK], start=True, stop=True
                       ).then_inc(s_g, 1)
                elif step[0] == "rows":
                    t = step[1]
                    R = t % NR
                    pe.wait_ge(s_h, t + 1)
                    if t >= 1:
                        pe.wait_ge(s_y, t)
                    for j in range(GB):
                        if t < NR:
                            last = mm(ps[:, 6, j * D:(j + 1) * D], work[D:P, 0, j * P:(j + 1) * P], w_12[D:P, 1, :],
                                      start=True, stop=True)
                        else:
                            last = mm(ps[:, 6, j * D:(j + 1) * D], hs[D:P, R * BLK + j * P:R * BLK + (j + 1) * P],
                                      ident[D:P, D:P], start=True, stop=True)
                    last.then_inc(s_r, 1)


_INS = ["x", "adj", "L0_gnn_W_u", "L0_gnn_diag_u", "L0_gnn_par_u", "L0_gnn_W_i", "L0_gnn_diag_i", "L0_gnn_par_i",
        "L0_gnn_ln_gamma", "L0_gnn_ln_beta", "L1_gnn_W1", "L1_gnn_wih1", "L1_gnn_whh1", "L1_gnn_bih1", "L1_gnn_bhh1",
        "L1_gnn_W2", "L1_gnn_wih2", "L1_gnn_whh2", "L1_gnn_bih2", "L1_gnn_bhh2"]
_OUTS = [((5120, 64), "float32")]


def kernel(**inputs):
    import numpy as _np
    import concourse.bacc as _bacc
    from concourse import mybir as _mybir
    from concourse.bass_utils import run_bass_kernel_spmd as _run

    nc = _bacc.Bacc("TRN2", target_bir_lowering=False, num_devices=1)
    arrays, args = {}, []
    for name in _INS:
        a = _np.ascontiguousarray(inputs[name])
        arrays[f"in_{name}_dram"] = a
        args.append(nc.dram_tensor(f"in_{name}_dram", a.shape, _mybir.dt.from_np(a.dtype), kind="ExternalInput").ap())
    for i, (shape, dtype) in enumerate(_OUTS):
        dt = _mybir.dt.from_np(_np.dtype(dtype))
        args.append(nc.dram_tensor(f"out_{i}_dram", shape, dt, kind="ExternalOutput").ap())
    bass_two_layer_gnn(nc, *args)
    r = _run(nc, [arrays], core_ids=[0])
    return r.results[0]["out_0_dram"]
```

```python
from contextlib import ExitStack

import concourse.bass as bass
from concourse import mybir

F32 = mybir.dt.float32
ALU = mybir.AluOpType
ACT = mybir.ActivationFunctionType
AX = mybir.AxisListType

P = 128
D = 64
N = 5120
G = N // P
CACHED = 4
BLK = 512
GB = BLK // P
NR = N // BLK
NK = (N - CACHED * P) // BLK
LN_EPS = 1e-5
USER_GROUPS = 16
PAIRS = 5
NSTAGE = 4
NTURN = 3
SB = 2 * P
NSB = N // SB
WIDE = 4
NB = NSB - 2 * WIDE
QUARTERS = ((0, 1), (2,), (3,), ())
PG = 8
NP = G // PG


SWEEP3 = [0, 9, 1, 8, 2, 7, 3, 6, 4, 5]
LAG = ({"sum": 2, "gates": 2, "state": 4, "rows": 6},
       {"sum": 1, "gates": 5, "state": 5, "rows": 7})


def block_of(t):
    return t if t < NR else SWEEP3[t - NR]


def plan_sweeps():
    steps, chunks, late = [], [], []
    done = 0
    for t in range(2 * NR):
        R = block_of(t)
        if t == 0:
            items = [0, 5, 1, 6, 2, 7, 3, 8, 4, "cached"]
        elif t < NR:
            items = [k for k in range(NK) if k != R - 1] + ["cached", R - 1]
        else:
            items = list(range(R, NK)) + ["cached"]
        if t >= 2:
            late.sort(key=lambda entry: entry[0])
            while any(step == ("sum", t - 2) for _, _, step in late):
                steps.append(late.pop(0)[2])
        for i, item in enumerate(items):
            if item == "cached":
                steps.append(("cached", t, R))
                done += 2
            else:
                steps.append(("chunk", len(chunks), t, R, item, i == 0))
                chunks.append((R, item))
                done += 4 if t < NR and item < R else 2
            late.sort(key=lambda entry: entry[0])
            while late and late[0][0] <= done:
                steps.append(late.pop(0)[2])
        due = done
        for name in ("sum", "gates", "state", "rows"):
            due += LAG[t >= NR][name]
            before = {"gates": "state"}.get(name, name)
            due = max([due] + [d + (name == "gates") for d, u, step in late if step == (before, t - 1)])
            late.append((due, t, (name, t)))
        if 0 < t < NR:
            late.append((due, t, ("second", t)))
    late.sort(key=lambda entry: entry[0])
    steps += [step for _, _, step in late]
    return steps, chunks


ONCE = ("diag", "coef", "weights", "keep_weights")


def skewed(stages, counts):
    order = [(kind, stage, i - lag) for i in range(PAIRS + max(s[2] for s in stages))
             for kind, stage, lag in stages if 0 <= i - lag < PAIRS and (kind not in ONCE or i == lag)]
    at = {}
    for engine, (start, per) in counts.items():
        n = start
        for step in order:
            if step[:2] in per:
                n += per[step[:2]]
                at[(engine,) + step] = n
        at[engine] = n
    return order, at

DVE_SETUP = 3

SETUP, setup_at = skewed(
    [("coef", "", 5), ("e", "", 6), ("diag", "", 4), ("prod", "", 5), ("turn", "", 4), ("keep", "", 4),
     ("norm", "d", 3), ("norm", "c", 2), ("norm", "b", 1), ("norm", "a", 0)],
    {"dve": (DVE_SETUP, {("norm", "a"): 3, ("norm", "c"): 1, ("norm", "d"): 2, ("coef", ""): 2, ("e", ""): 2}),
     "act": (0, {("norm", "b"): 1, ("norm", "c"): 1, ("norm", "d"): 1, ("keep", ""): 1}),
     "pe": (0, {("diag", ""): 1, ("turn", ""): 1, ("prod", ""): 1})})
MIDDLE, mid_at = skewed(
    [("keep_y", "", 10), ("y", "", 9), ("turn", "", 8), ("keep", "", 8), ("norm2", "d", 7), ("norm2", "c", 6),
     ("norm2", "b", 5), ("norm2", "a", 4), ("residual", "", 3), ("norm1", "d", 2), ("norm1", "c", 1),
     ("hrows", "", 0), ("norm1", "b", 0), ("weights", "", 1), ("keep_weights", "", 1)],
    {"dve": (0, {("keep_weights", ""): 1, ("norm1", "c"): 1, ("norm1", "d"): 2, ("norm2", "a"): 2, ("norm2", "c"): 1,
                 ("norm2", "d"): 2, ("keep_y", ""): 1}),
     "act": (PAIRS, {("norm1", "b"): 1, ("norm1", "c"): 1, ("norm2", "b"): 1, ("norm2", "c"): 1, ("keep", ""): 4}),
     "pool": (3 * PAIRS, {("residual", ""): 2, ("norm2", "a"): 1}),
     "pe": (0, {("hrows", ""): 1, ("weights", ""): 1, ("turn", ""): 1, ("y", ""): 1})})


class Count:

    def __init__(self, sem):
        self.sem, self.n = sem, 0

    def up(self, instruction, by=1):
        self.n += by
        instruction.then_inc(self.sem, by)
        return self.n


def bass_two_layer_gnn(nc, x, adj, W_u, diag_u, par_u, W_i, diag_i, par_i, gamma, beta,
                       W1, wih1, whh1, bih1, bhh1, W2, wih2, whh2, bih2, bhh2, out):
    steps, chunks = plan_sweeps()
    POOL_X = 3 * PAIRS
    with ExitStack() as ctx:
        def sb(name, shape):
            return ctx.enter_context(nc.sbuf_tensor(name, shape, F32))

        def sem(name):
            return ctx.enter_context(nc.semaphore(name))

        at = sb("at", [P, CACHED, N])
        arena = sb("arena", [P, 14336])
        xs = sb("xs", [P, G, D])
        es = sb("es", [P, G, D])
        y1 = sb("y1", [P, G, D])
        hs = sb("hs", [P, N])
        work = sb("work", [P, 5, BLK])
        outs = sb("outs", [P, 2, GB * D])
        ident = sb("ident", [P, P])
        twice = sb("twice", [P, D])
        w_ui = sb("w_ui", [P, 2, P])
        w_11 = sb("w_11", [P, P])
        w_rz = sb("w_rz", [P, 2, P])
        w_n = sb("w_n", [P, 2, P])
        w_2 = sb("w_2", [P, D])
        gam = sb("gam", [P, D])
        bet = sb("bet", [P, D])
        b_ih = sb("b_ih", [P, 2, 2])
        b_hh = sb("b_hh", [P, 2, 2])
        b_rz = sb("b_rz", [P, 2])
        par = sb("par", [P, 2, 2])
        parp = sb("parp", [P, 2])
        dT = sb("dT", [G, P])
        coef = sb("coef", [P, G])
        eps = sb("eps", [P, 1])
        stat = sb("stat", [P, PAIRS, 4, 8])
        zT = sb("zT", [P, SB])
        zs = sb("zs", [P, 2, 2, D])
        centre = sb("centre", [P, P])

        piece = arena[:, 0:G * SB].rearrange("p (s g c) -> p s g c", s=NP, g=PG)
        incoming = arena[:, 0:NSTAGE * 2048].rearrange("p (s f) -> p s f", s=NSTAGE)
        turned = arena[:, NSTAGE * 2048:(NSTAGE + NTURN) * 2048].rearrange("p (s j i) -> p s j i", s=NTURN, j=GB)
        wide_in = arena[:, G * SB:].rearrange("p (s f) -> p s f", s=2)
        wide_turned = hs[:, 0:4096].rearrange("p (s j i) -> p s j i", s=2, j=GB)
        wide_zT = work[:, 0, :]
        wide_z = y1[:, 0:16, :].rearrange("p (k j) d -> p k j d", k=WIDE)
        wide_now = y1[:, 16:20, :]
        raw = y1[:, 32:40, :].rearrange("p (w h) d -> p w h d", w=4)
        h0T = y1[:, 0:16, :].rearrange("p (s g) d -> p s (g d)", s=2)
        hT = es[:].rearrange("p g d -> p (g d)")
        y2 = es
        scratch = [hs[:, :].rearrange("p (s f) -> p s f", s=10),
                   arena[:, NSTAGE * 2048:NSTAGE * 2048 + 5120].rearrange("p (s f) -> p s f", s=10)]

        ps = ctx.enter_context(nc.psum_tensor("ps", [P, 8, BLK], F32))
        Z_BANK, TP_BANK = 5, 6

        s_x = [sem(f"x_chunk_loaded_{c}") for c in range(PAIRS)]
        s_w = sem("weights_loaded")
        s_idg = sem("identity_on_pool")
        s_id = sem("identity_ready")
        s_dve = sem("dve_steps")
        s_dve2 = sem("dve_mid_steps")
        s_act = sem("act_steps")
        s_act2 = sem("act_mid_steps")
        s_pe = sem("pe_setup_steps")
        s_pe2 = sem("pe_mid_steps")
        s_pool = sem("pool_steps")
        s_dw = sem("gru_weights_loaded")
        s_piece = [sem(f"piece_loaded_{i}") for i in range(NP)]
        s_pu = sem("pieces_used")
        s_tp = sem("transposes_done")
        s_ta = sem("transposes_kept_by_act")
        s_tv = sem("transposes_kept_by_dve")
        s_zc = sem("z_transposed_copied")
        s_zn = sem("z_rows_done")
        s_z = sem("z_ready")
        s_wl = [sem(f"wide_chunk_loaded_{i}") for i in range(2)]
        s_wt = sem("wide_chunks_transposed")
        s_wu = sem("wide_chunks_used")
        s_wz = sem("wide_z_copied")
        s_p2 = sem("block_product_done")
        s_stage = [sem(f"chunk_loaded_{i}") for i in range(NSTAGE)]
        s_turn = sem("chunk_transposed")
        s_used = sem("chunk_used")
        s_m1 = sem("product_done")
        s_mt = sem("upper_half_moved")
        s_m = sem("product_kept")
        s_g = sem("gates_done")
        s_rz = sem("sigmoid_done")
        s_u = sem("tanh_input_ready")
        s_n = sem("tanh_done")
        s_hv = sem("new_state_ready")
        s_h = sem("new_state_kept")
        s_r = sem("rows_done")
        s_y = sem("rows_kept")
        s_m2t = sem("second_upper_half_moved")
        s_m2k = sem("second_product_kept")
        s_gd = sem("gate_steps")
        s_out = [sem(f"stored_{i}") for i in range(2)]

        weight_loads = [
            (dT[0:USER_GROUPS, :], diag_u.rearrange("(g p) -> g p", p=P)),
            (dT[USER_GROUPS:G, :], diag_i.rearrange("(g p) -> g p", p=P)),
            (par[:, 0, :], par_u.partition_broadcast(P)),
            (par[:, 1, :], par_i.partition_broadcast(P)),
            (w_ui[0:D, 0, 0:D], W_u), (w_ui[D:P, 0, D:P], W_i),
            (w_ui[0:D, 1, 0:D], W_i), (w_ui[D:P, 1, D:P], W_i),
            (gam[:], gamma.partition_broadcast(P)), (bet[:], beta.partition_broadcast(P)),
        ]
        gru_loads = [(w_11[0:D, 0:D], W1), (w_11[D:P, D:P], W1), (w_2[D:P, :], W2)]
        for w, m in enumerate((wih1, whh1, wih2, whh2)):
            gru_loads += [(raw[:, w, 0, :], m[0:P, :]), (raw[0:D, w, 1, :], m[P:3 * D, :])]
        for l, (bi, bh) in enumerate(((bih1, bhh1), (bih2, bhh2))):
            gru_loads += [
                (b_ih[:, l, 0:1], bi[0:P].rearrange("(p o) -> p o", o=1)),
                (b_hh[:, l, 0:1], bh[0:P].rearrange("(p o) -> p o", o=1)),
                (b_ih[D:P, l, 1:2], bi[P:3 * D].rearrange("(p o) -> p o", o=1)),
                (b_hh[0:D, l, 1:2], bh[P:3 * D].rearrange("(p o) -> p o", o=1)),
            ]
        WEIGHTS_IN = 16 * len(weight_loads)
        GRU_IN = 16 * len(gru_loads)

        def pair(buf, c):
            return buf[:].rearrange("p (h g) d -> p h g d", h=2)[:, :, 4 * c:4 * c + 4, :]

        def eight(ap):
            return ap.rearrange("p (h g d) -> p h g d", h=2, g=4)

        def mixed(ap):
            return ap.rearrange("p (g h d) -> p h g d", h=2, g=4)

        def spread(col):
            return col.rearrange("p (h g o) -> p h g o", h=2, o=1).broadcast_to([P, 2, 4, D])

        def spread3(col):
            return col.rearrange("p (g o) -> p g o", o=1).broadcast_to([P, 8, D])

        def rows_of(row):
            return row.rearrange("p (g d) -> p g d", g=1).broadcast_to([P, 8, D])

        def group_of(c, i):
            return 4 * c + i if i < 4 else 20 + 4 * c + i - 4

        def in_group_order(R, natural):
            if R * GB >= G - CACHED:
                return natural.rearrange("p (q j b) -> p q j b", q=4, b=32)
            return natural.rearrange("p (j q b) -> p q j b", q=4, b=32)

        def quarters_of_groups(natural):
            return natural.rearrange("p (j q b) -> p q j b", q=4, b=32)

        def quarters(ap):
            return ap.rearrange("p (q j b) -> p q j b", q=4, b=32)

        last_of = {s[2 if s[0] == "chunk" else 1]: s for s in steps if s[0] in ("chunk", "cached")}

        block = ctx.enter_context(nc.Block())

        @block.sync
        def _(sp):
            for c in range(PAIRS):
                for h in range(2):
                    g0 = 20 * h + 4 * c
                    sp.dma_start(xs[:, g0:g0 + 4, :], x[g0 * P:(g0 + 4) * P, :].rearrange("(g p) d -> p g d", p=P)
                                 ).then_inc(s_x[c], 16)
                if c == 0:
                    sp.wait_ge(s_dve, DVE_SETUP)
                    for dst, src in weight_loads:
                        sp.dma_start(dst, src).then_inc(s_w, 16)

            def load_piece(i, column):
                sp.dma_start(piece[:, i], adj[PG * P * i:PG * P * (i + 1), bass.ds(column, SB)].rearrange(
                    "(g p) c -> p g c", p=P)).then_inc(s_piece[i], 16)

            def load_wide_chunks(m, column):
                for h in range(2):
                    rows = adj[(m + 5 * h) * BLK:(m + 5 * h + 1) * BLK, :].rearrange("(i a) c -> a i c", a=32)
                    for q in range(4):
                        sp.dma_start(wide_in[32 * q:32 * q + 32, h].rearrange("p (i c) -> p i c", c=P),
                                     rows[:, :, bass.ds(column + q * P, P)]).then_inc(s_wl[h], 16)

            load = 0
            for b in range(WIDE):
                for column in (b * BLK, b * BLK + SB, WIDE * BLK + b * SB):
                    for i in range(NP):
                        if load:
                            sp.wait_ge(s_pu, (load - 1) * NP + i + 1)
                        load_piece(i, column)
                    load += 1
            with sp.Fori(WIDE, NB - 1, 2) as b:
                for what in ("p0", "p1", "p2", "w0", "p3", "p4", "w1", "p5", "p6", "w2", "p7", "p8", "w3", "p9", "w4"):
                    i = int(what[1])
                    if what[0] == "p":
                        sp.wait_ge(s_pu, b * NP + (2 * WIDE * NP + i + 1 - NP))
                        load_piece(i % NP, b * SB + (2 * WIDE + i // NP) * SB)
                    else:
                        sp.wait_ge(s_wt, b * 10 + (4 * i + 2 - 10 * WIDE))
                        load_wide_chunks(i, b * SB - WIDE * SB)

            sp.wait_ge(s_pu, NP * NSB)
            for n, (R, k) in enumerate(chunks):
                slot = n % NSTAGE
                if n >= NSTAGE:
                    sp.wait_ge(s_turn, n - NSTAGE + 1)
                rows = adj[R * BLK:(R + 1) * BLK, :].rearrange("(i a) c -> a i c", a=32)
                for q in range(4):
                    sp.dma_start(incoming[32 * q:32 * q + 32, slot].rearrange("p (i c) -> p i c", c=P),
                                 rows[:, :, k * BLK + q * P:k * BLK + (q + 1) * P]).then_inc(s_stage[slot], 16)

        @block.gpsimd
        def _(pool):
            own = Count(s_idg)
            n = own.up(nc.gpsimd.memset(ident[:], 0.0))
            pool.wait_ge(s_idg, n)
            n = own.up(nc.gpsimd.affine_select(out=ident[:], in_=ident[:], compare_op=ALU.not_equal, fill=1.0, base=0,
                                               pattern=[[-1, P]], channel_multiplier=1))
            pool.wait_ge(s_dve, DVE_SETUP)
            pool.wait_ge(s_idg, n)
            nc.gpsimd.tensor_tensor(twice[:], ident[:, 0:D], ident[:, D:P], ALU.add)
            nc.gpsimd.tensor_tensor(centre[:], centre[:], ident[:], ALU.add).then_inc(s_id, 1)
            pool.wait_ge(s_w, WEIGHTS_IN)
            done = Count(s_pool)
            for c in range(PAIRS):
                pool.wait_ge(s_act, setup_at["act", "norm", "d", c])
                xv = pair(xs, c)
                n = done.up(nc.gpsimd.tensor_tensor(xv, xv, mixed(scratch[0][:, 5 + c, :]), ALU.add))
                pool.wait_ge(s_pool, n)
                for h in range(2):
                    v = xs[:, 20 * h + 4 * c:20 * h + 4 * c + 4, :]
                    done.up(nc.gpsimd.tensor_tensor(
                        v, v, bet[:].rearrange("p (g d) -> p g d", g=1).broadcast_to([P, 4, D]), ALU.add))

            pool.wait_ge(s_z, 2 * WIDE - 1)
            nc.gpsimd.tensor_copy(wide_now[:].rearrange("p g d -> p (g d)"),
                                  y1[:, 0:GB, :].rearrange("p g d -> p (g d)")).then_inc(s_wz, 2)
            with pool.Fori(1, WIDE) as k:
                pool.wait_ge(s_wu, k * 10 + 2)
                nc.gpsimd.tensor_copy(wide_now[:].rearrange("p g d -> p (g d)"),
                                      y1[:, 0:16, :].rearrange("p g d -> p (g d)")[:, bass.ds(k * GB * D, GB * D)]
                                      ).then_inc(s_wz, 2)

            sc = scratch[1]
            for kind, stage, c in MIDDLE:
                if kind == "residual":
                    pool.wait_ge(s_dve2, mid_at["dve", "norm1", "d", c])
                    v = sc[:, c, :].rearrange("p (g d) -> p g d", d=D)
                    n = done.up(nc.gpsimd.tensor_tensor(v, v, rows_of(gam[:]), ALU.mult))
                    pool.wait_ge(s_pool, n)
                    done.up(nc.gpsimd.tensor_tensor(pair(xs, c), mixed(sc[:, c, :]), pair(xs, c), ALU.add))
                elif kind == "norm2" and stage == "a":
                    pool.wait_ge(s_dve2, mid_at["dve", "norm2", "a", c])
                    pool.wait_ge(s_pool, mid_at["pool", "residual", "", c])
                    done.up(nc.gpsimd.tensor_tensor(mixed(sc[:, c, :]), pair(xs, c), spread(stat[:, c, 0, :]),
                                                    ALU.add))

            for step in steps:
                if step[0] == "state":
                    t = step[1]
                    R = block_of(t)
                    pool.wait_ge(s_n, t + 1)
                    n = done.up(nc.gpsimd.tensor_tensor(work[D:P, 2, :], hs[D:P, R * BLK:(R + 1) * BLK],
                                                        work[D:P, 3, :], ALU.subtract))
                    pool.wait_ge(s_pool, n)
                    n = done.up(nc.gpsimd.tensor_tensor(work[D:P, 2, :], work[D:P, 2, :], work[D:P, 1, :], ALU.mult))
                    pool.wait_ge(s_pool, n)
                    nc.gpsimd.tensor_tensor(work[D:P, 2, :], work[D:P, 2, :], work[D:P, 3, :], ALU.add
                                            ).then_inc(s_hv, 1)

        @block.scalar
        def _(act):
            def squares(c, s_a, sc):
                nc.scalar.activation(sc[:, 5 + c, :], sc[:, c, :], ACT.Square).then_inc(s_a, 1)

            def deviation(c, s_a):
                nc.scalar.activation(stat[:, c, 2, :], stat[:, c, 1, :], ACT.Sqrt, bias=eps[:], scale=1.0 / D
                                     ).then_inc(s_a, 1)

            for kind, stage, c in SETUP:
                if kind == "norm" and stage == "b":
                    act.wait_ge(s_dve, setup_at["dve", "norm", "a", c])
                    squares(c, s_act, scratch[0])
                elif kind == "norm" and stage == "c":
                    act.wait_ge(s_dve, setup_at["dve", "norm", "c", c])
                    deviation(c, s_act)
                elif kind == "norm" and stage == "d":
                    act.wait_ge(s_dve, setup_at["dve", "norm", "d", c])
                    nc.scalar.activation(scratch[0][:, 5 + c, :], scratch[0][:, c, :], ACT.Relu).then_inc(s_act, 1)
                elif kind == "keep":
                    act.wait_ge(s_pe, setup_at["pe", "turn", "", c])
                    if c >= 2:
                        act.wait_ge(s_pe, setup_at["pe", "prod", "", c - 2])
                    nc.scalar.activation(h0T[:, c % 2, :], ps[:, c % 2, :], ACT.Copy).then_inc(s_act, 1)

            act.wait_ge(s_dve, DVE_SETUP)
            for dst, src in gru_loads:
                act.dma_start(dst, src).then_inc(s_dw, 16)

            def keep_z(n, rows):
                act.wait_ge(s_zn, n + 1)
                nc.scalar.activation(rows.rearrange("p j d -> p (j d)"),
                                     ps[:, TP_BANK + 1, 0:rows.shape[1] * D], ACT.Copy).then_inc(s_z, 1)

            def keep_transposes(b, slot, z_before=None):
                for s in range(10):
                    act.wait_ge(s_tp, b * 20 + (2 * s + 1))
                    if s == 0 and (not isinstance(b, int) or b >= 2):
                        act.wait_ge(s_p2, b - 1)
                    nc.scalar.activation(at[:, 2 * slot, s * BLK:(s + 1) * BLK], ps[:, TP_BANK, :], ACT.Copy
                                         ).then_inc(s_ta, 1)
                    if s == 0:
                        keep_z(*z_before)

            for b in range(WIDE):
                if b:
                    keep_z(2 * b - 1, zs[:, (b - 1) % 2])
                keep_transposes(b, b % 2, (2 * b, wide_z[:, b]))
            with act.Fori(WIDE, NB - 1, 2) as b:
                for i in range(2):
                    keep_transposes(b + i, i, (b + (WIDE + i - 1), zs[:, 1 - i]))
            keep_z(NB + WIDE - 1, zs[:, (NB - 1) % 2])

            for c in range(PAIRS):
                act.wait_ge(s_p2, NB + c)
                nc.scalar.activation(hT[:, c * BLK:(c + 1) * BLK], ps[:, c, :], ACT.Copy).then_inc(s_act2, 1)
            for kind, stage, c in MIDDLE:
                if kind == "norm1" and stage == "b":
                    act.wait_ge(s_pe2, mid_at["pe", "hrows", "", c])
                    nc.scalar.activation(scratch[1][:, 5 + c, :], ps[:, 6 + c % 2, :], ACT.Square
                                         ).then_inc(s_act2, 1)
                elif kind == "norm2" and stage == "b":
                    act.wait_ge(s_pool, mid_at["pool", "norm2", "a", c])
                    squares(c, s_act2, scratch[1])
                elif kind in ("norm1", "norm2") and stage == "c":
                    act.wait_ge(s_dve2, mid_at["dve", kind, "c", c])
                    deviation(c, s_act2)
                elif kind == "keep":
                    act.wait_ge(s_pe2, mid_at["pe", "turn", "", c])
                    if c >= 2:
                        act.wait_ge(s_pe2, mid_at["pe", "y", "", c - 2])
                    for h in range(2):
                        nc.scalar.activation(hs[D:P, (c + 5 * h) * BLK:(c + 5 * h + 1) * BLK],
                                             ps[D * h:D * h + D, 4 + c % 2, :], ACT.Relu).then_inc(s_act2, 1)
                        half = slice(D * h, D * h + D)
                        nc.scalar.activation(in_group_order(c + 5 * h, work[half, c % 2, :]),
                                             quarters(ps[half, 4 + c % 2, :]), ACT.Relu).then_inc(s_act2, 1)

            for step in steps:
                if step[0] == "sum":
                    t = step[1]
                    act.wait_ge(s_m1, t + 1)
                    if t > 0:
                        act.wait_ge(s_m, t)
                    nc.scalar.activation(work[0:D, 0, :], ps[D:P, t % 2, :], ACT.Copy).then_inc(s_mt, 1)
                elif step[0] == "gates":
                    t = step[1]
                    act.wait_ge(s_g, t + 1)
                    if t > 0:
                        act.wait_ge(s_hv, t)
                    nc.scalar.activation(work[:, 1, :], ps[:, 4, :], ACT.Sigmoid, bias=b_rz[:, t // NR:t // NR + 1]
                                         ).then_inc(s_rz, 1)
                elif step[0] == "state":
                    t = step[1]
                    l, R = t // NR, block_of(t)
                    cols = slice(R * BLK, (R + 1) * BLK)
                    act.wait_ge(s_u, t + 1)
                    nc.scalar.activation(work[D:P, 3, :], work[D:P, 2, :], ACT.Tanh, bias=b_ih[D:P, l, 1:2]
                                         ).then_inc(s_n, 1)
                    act.wait_ge(s_hv, t + 1)
                    if t < NR:
                        nc.scalar.activation(hs[D:P, cols], work[D:P, 2, :], ACT.Relu)
                        nc.scalar.activation(in_group_order(R, work[D:P, 0, :]), quarters(work[D:P, 2, :]), ACT.Relu
                                             ).then_inc(s_h, 1)
                    else:
                        nc.scalar.activation(hs[D:P, cols], work[D:P, 2, :], ACT.Relu).then_inc(s_h, 1)
                elif step[0] == "rows":
                    t = step[1]
                    R = block_of(t)
                    if t < NR:
                        act.wait_ge(s_r, t + 1)
                        nc.scalar.activation(y2[:, GB * R:GB * R + GB, :].rearrange("p g d -> p (g d)"),
                                             ps[:, 6, 0:GB * D], ACT.Copy).then_inc(s_y, 1)
                    else:
                        act.wait_ge(s_y, t + 1)
                        act.dma_start(out[R * BLK:(R + 1) * BLK, :].rearrange("(g p) d -> p g d", p=P),
                                      outs[:, t % 2, :].rearrange("p (g d) -> p g d", d=D)
                                      ).then_inc(s_out[t % 2], 16)
                elif step[0] == "second":
                    R = step[1]
                    act.wait_ge(s_used, last_of[R][1] + 1)
                    if R > 1:
                        act.wait_ge(s_m2k, R - 1)
                    nc.scalar.activation(work[0:D, 4, :], ps[D:P, 2 + R % 2, :], ACT.Copy).then_inc(s_m2t, 1)
            for i in range(2):
                act.wait_ge(s_out[i], 16 * (NR // 2))

        @block.vector
        def _(dve):
            own = Count(s_dve)
            own.up(nc.vector.memset(eps[:], LN_EPS))
            nc.vector.memset(w_ui[:], 0.0).then_inc(s_wt, 2)
            nc.vector.memset(w_11[:], 0.0)
            own.up(nc.vector.memset(w_n[:], 0.0))
            for h in range(2):
                nc.vector.memset(centre[D * h:D * h + D, D * (1 - h):D * (1 - h) + D], 0.0)
                last = nc.vector.memset(centre[D * h:D * h + D, D * h:D * h + D], -1.0 / D)
            own.up(last)
            assert own.n == DVE_SETUP

            def sum_of_squares(cnt, c, sc):
                cnt.up(nc.vector.tensor_reduce(stat[:, c, 1, :], mixed(sc[:, 5 + c, :]), AX.X, ALU.add))

            def minus_mean(cnt, c, src):
                n = cnt.up(nc.vector.tensor_reduce(stat[:, c, 0, :], src, AX.X, ALU.add))
                dve.wait_ge(cnt.sem, n)
                return cnt.up(nc.vector.tensor_scalar(stat[:, c, 0, :], stat[:, c, 0, :], -1.0 / D, None, ALU.mult))

            def scaled(cnt, c, src, sc):
                n = cnt.up(nc.vector.reciprocal(stat[:, c, 3, :], stat[:, c, 2, :]))
                dve.wait_ge(cnt.sem, n)
                cnt.up(nc.vector.tensor_tensor(mixed(sc[:, c, :]), src, spread(stat[:, c, 3, :]), ALU.mult))

            for kind, stage, c in SETUP:
                if kind == "norm" and stage == "a":
                    dve.wait_ge(s_x[c], 32)
                    n = minus_mean(own, c, pair(xs, c))
                    dve.wait_ge(s_dve, n)
                    own.up(nc.vector.tensor_tensor(mixed(scratch[0][:, c, :]), pair(xs, c), spread(stat[:, c, 0, :]),
                                                   ALU.add))
                elif kind == "norm" and stage == "c":
                    dve.wait_ge(s_act, setup_at["act", "norm", "b", c])
                    sum_of_squares(own, c, scratch[0])
                elif kind == "norm" and stage == "d":
                    dve.wait_ge(s_act, setup_at["act", "norm", "c", c])
                    scaled(own, c, mixed(scratch[0][:, c, :]), scratch[0])
                elif kind == "coef":
                    dve.wait_ge(s_w, WEIGHTS_IN)
                    n = own.up(nc.vector.tensor_tensor(parp[:], par[:, :, 0], par[:, :, 1], ALU.mult))
                    dve.wait_ge(s_dve, n)
                    dve.wait_ge(s_pe, setup_at["pe", "diag", "", 0])
                    nc.vector.tensor_scalar(coef[:, 0:USER_GROUPS], ps[:, 7, 0:USER_GROUPS], parp[:, 0:1], None,
                                            ALU.mult)
                    n = own.up(nc.vector.tensor_scalar(coef[:, USER_GROUPS:G], ps[:, 7, USER_GROUPS:G], parp[:, 1:2],
                                                       None, ALU.mult))
                    dve.wait_ge(s_dve, n)
                elif kind == "e":
                    dve.wait_ge(s_pe, setup_at["pe", "prod", "", c])
                    scale = coef[:].rearrange("p (h g o) -> p h g o", h=2, o=1)[:, :, 4 * c:4 * c + 4, :]
                    last = nc.vector.tensor_tensor(pair(es, c), mixed(ps[:, 4, :]), scale.broadcast_to([P, 2, 4, D]),
                                                   ALU.mult)
                    n = own.up(last)
                    dve.wait_ge(s_dve, n)
                    own.up(nc.vector.tensor_tensor(pair(es, c), pair(es, c), mixed(scratch[0][:, 5 + c, :]), ALU.add))
            assert own.n == setup_at["dve"]

            def keep_transposes(b, slot, quarters_at=None):
                for s in range(10):
                    dve.wait_ge(s_tp, b * 20 + (2 * s + 2))
                    if s == 0 and (not isinstance(b, int) or b >= 2):
                        dve.wait_ge(s_p2, b - 1)
                    nc.vector.tensor_copy(at[:, 2 * slot + 1, s * BLK:(s + 1) * BLK], ps[:, TP_BANK + 1, :]
                                          ).then_inc(s_tv, 1)
                    for quarter in (quarters_at or {}).get(s, ()):
                        turn_wide_quarter(b - slot, *quarter)

            def turn_wide_quarter(b, m, quarter):
                h, half = quarter // 2, quarter % 2
                if quarter == 0:
                    dve.wait_ge(s_wu, b * 5 + (2 * m + 2 - 5 * WIDE))
                if half == 0:
                    dve.wait_ge(s_wl[h], b * 160 + (64 * m + 64 - 160 * WIDE))
                nc.vector.transpose(
                    wide_turned[:, h, :, 256 * half:256 * half + 256].rearrange("p j (i a) -> p i j a", a=32),
                    wide_in[:, h, 1024 * half:1024 * half + 1024].rearrange("p (i j b) -> p i j b", j=GB, b=32)
                    ).then_inc(s_wt, 1)

            def keep_zT(loads):
                dve.wait_ge(s_pu, loads * NP)
                nc.vector.tensor_copy(zT[:], ps[:, Z_BANK, 0:SB]).then_inc(s_zc, 1)

            for b in range(WIDE):
                if b:
                    keep_zT(3 * b)
                dve.wait_ge(s_pu, (3 * b + 2) * NP)
                nc.vector.tensor_copy(quarters_of_groups(wide_zT), quarters(ps[:, Z_BANK, :])).then_inc(s_zc, 1)
                keep_transposes(b, b % 2)
            def wide_quarters(i):
                return {s: [((10 * i + s) // 4, q) for q in QUARTERS[(10 * i + s) % 4]] for s in range(10)}

            dve.wait_ge(s_pool, POOL_X)
            with dve.Fori(WIDE, NB - 1, 2) as b:
                for i in range(2):
                    keep_zT(b + (2 * WIDE + i))
                    keep_transposes(b + i, i, wide_quarters(i))
            keep_zT(NSB)

            mid = Count(s_dve2)
            sc = scratch[1]
            for kind, stage, c in MIDDLE:
                if kind == "keep_weights":
                    dve.wait_ge(s_pe2, mid_at["pe", "weights", "", 0])
                    nc.vector.tensor_tensor(b_rz[:], b_ih[:, :, 0], b_hh[:, :, 0], ALU.add)
                    for l in range(2):
                        nc.vector.tensor_copy(w_rz[:, l, :], ps[:, 5, l * 2 * P:l * 2 * P + P])
                        nc.vector.tensor_copy(w_n[0:D, l, D:P], ps[0:D, 5, l * 2 * P + P + D:l * 2 * P + 2 * P])
                        last = nc.vector.tensor_copy(w_n[D:P, l, 0:D], ps[D:P, 5, l * 2 * P + P:l * 2 * P + P + D])
                    mid.up(last)
                elif kind in ("norm1", "norm2") and stage == "c":
                    dve.wait_ge(s_act2, mid_at["act", kind, "b", c])
                    sum_of_squares(mid, c, sc)
                elif kind == "norm1" and stage == "d":
                    dve.wait_ge(s_act2, mid_at["act", "norm1", "c", c])
                    scaled(mid, c, ps[:, 6 + c % 2, :].rearrange("p (g h d) -> p h g d", h=2, d=D), sc)
                elif kind == "norm2" and stage == "a":
                    dve.wait_ge(s_pool, mid_at["pool", "residual", "", c])
                    minus_mean(mid, c, pair(xs, c))
                elif kind == "norm2" and stage == "d":
                    dve.wait_ge(s_act2, mid_at["act", "norm2", "c", c])
                    scaled(mid, c, mixed(sc[:, c, :]), sc)
                elif kind == "keep_y":
                    dve.wait_ge(s_pe2, mid_at["pe", "y", "", c])
                    mid.up(nc.vector.tensor_copy(pair(y1, c), mixed(ps[:, 3, :])))
            assert mid.n == mid_at["dve"]

            def turn_chunk(n):
                slot, to = n % NSTAGE, n % NTURN
                dve.wait_ge(s_stage[slot], 64 * (n // NSTAGE + 1))
                if n >= NTURN:
                    dve.wait_ge(s_used, n - NTURN + 1)
                nc.vector.transpose(turned[:, to].rearrange("p j (i a) -> p i j a", a=32),
                                    incoming[:, slot].rearrange("p (i j b) -> p i j b", j=GB, b=32)
                                    ).then_inc(s_turn, 1)

            g = Count(s_gd)
            dve.wait_ge(s_pe2, mid_at["pe", "turn", "", PAIRS - 1])
            turn_chunk(0)
            turn_chunk(1)
            for step in steps:
                if step[0] == "chunk":
                    if step[1] + 2 < len(chunks):
                        turn_chunk(step[1] + 2)
                elif step[0] == "sum":
                    t = step[1]
                    R = block_of(t)
                    cols = slice(R * BLK, (R + 1) * BLK)
                    dve.wait_ge(s_mt, t + 1)
                    if t >= NR and R > 0:
                        n = g.up(nc.vector.tensor_tensor(work[0:D, 0, :], work[0:D, 0, :], hs[0:D, cols], ALU.add))
                        dve.wait_ge(s_gd, n)
                    nc.vector.tensor_tensor(hs[0:D, cols], ps[0:D, t % 2, :], work[0:D, 0, :], ALU.add
                                            ).then_inc(s_m, 1)
                elif step[0] == "gates":
                    t = step[1]
                    l = t // NR
                    dve.wait_ge(s_rz, t + 1)
                    n = g.up(nc.vector.scalar_tensor_tensor(out=work[D:P, 2, :], in0=ps[0:D, 5, :],
                                                            scalar=b_hh[0:D, l, 1:2], in1=work[0:D, 1, :],
                                                            op0=ALU.add, op1=ALU.mult))
                    dve.wait_ge(s_gd, n)
                    nc.vector.tensor_tensor(work[D:P, 2, :], ps[D:P, 5, :], work[D:P, 2, :], ALU.add
                                            ).then_inc(s_u, 1)
                elif step[0] == "rows" and step[1] >= NR:
                    t = step[1]
                    R = block_of(t)
                    dve.wait_ge(s_r, t + 1)
                    if t >= NR + 2:
                        dve.wait_ge(s_out[t % 2], 16 * ((t - NR) // 2))
                    nc.vector.tensor_tensor(outs[:, t % 2, :], ps[:, 6, 0:GB * D],
                                            xs[:, GB * R:GB * R + GB, :].rearrange("p g d -> p (g d)"), ALU.add
                                            ).then_inc(s_y, 1)
                elif step[0] == "second":
                    R = step[1]
                    dve.wait_ge(s_m2t, R)
                    nc.vector.tensor_tensor(hs[0:D, R * BLK:(R + 1) * BLK], ps[0:D, 2 + R % 2, :], work[0:D, 4, :],
                                            ALU.add).then_inc(s_m2k, 1)

        @block.tensor
        def _(pe):
            mm = nc.tensor.matmul
            pe.wait_ge(s_id, 1)
            for kind, _, c in SETUP:
                if kind == "turn":
                    pe.wait_ge(s_act, setup_at["act", "norm", "d", c])
                    if c >= 2:
                        pe.wait_ge(s_act, setup_at["act", "keep", "", c - 2])
                    for i in range(4):
                        last = nc.tensor.transpose(ps[:, c % 2, i * P:(i + 1) * P],
                                                   scratch[0][:, 5 + c, i * P:(i + 1) * P], ident[:])
                        if c == 0 and i == 0:
                            last.then_inc(s_wu, 2)
                    last.then_inc(s_pe, 1)
                elif kind == "diag":
                    pe.wait_ge(s_w, WEIGHTS_IN)
                    mm(ps[:, 7, 0:G], dT[:, :], ident[0:G, 0:G], start=True, stop=True).then_inc(s_pe, 1)
                elif kind == "prod":
                    pe.wait_ge(s_act, setup_at["act", "keep", "", c])
                    if c:
                        pe.wait_ge(s_dve, setup_at["dve", "e", "", c - 1])
                    for i in range(GB):
                        last = mm(ps[:, 4, i * P:(i + 1) * P], h0T[:, c % 2, i * P:(i + 1) * P],
                                  w_ui[:, 0 if 4 * c + i < USER_GROUPS else 1, :], start=True, stop=True)
                    last.then_inc(s_pe, 1)

            def h_products(slot, half, s, first, last_block):
                bank, j = s // 2, s % 2
                for h in range(2):
                    done = mm(ps[D * h:D * h + D, bank, :], zs[:, half, j, :],
                              at[:, 2 * slot + j, (h * 5 + bank) * BLK:(h * 5 + bank + 1) * BLK],
                              start=first and j == 0, stop=last_block and j == 1, skip_group_check=True)
                return done

            def z_rows(n, rows_T):
                pe.wait_ge(s_zc, n + 1)
                for j in range(rows_T.shape[1] // P):
                    last = mm(ps[:, TP_BANK + 1, j * D:(j + 1) * D], rows_T[:, j * P:(j + 1) * P], twice[:],
                              start=True, stop=True, skip_group_check=True)
                last.then_inc(s_zn, 1)

            def turn_quad(s, j):
                for i in range(4):
                    g = 4 * s + i
                    last = nc.tensor.transpose(ps[:, TP_BANK + j, i * P:(i + 1) * P],
                                               piece[:, g // PG, g % PG, j * P:(j + 1) * P], ident[:])
                last.then_inc(s_tp, 1)

            def z_products(s, o):
                for i in range(4):
                    g = 4 * s + i
                    last = mm(ps[D * (g % 2):D * (g % 2) + D, Z_BANK, o:o + SB], es[:, g, :],
                              piece[:, g // PG, g % PG, :], start=g < 2, stop=g >= G - 2, skip_group_check=True)
                if s % 2 == 1:
                    last.then_inc(s_pu, 1)

            def wide_block(b):
                if b:
                    pe.wait_ge(s_tv, b * 10)
                    z_rows(2 * b - 1, zT)
                for half in range(2):
                    for s in range(10):
                        if s % 2 == 0:
                            pe.wait_ge(s_piece[s // 2], (3 * b + half) * 16 + 16)
                        z_products(s, half * SB)
                if b:
                    pe.wait_ge(s_z, 2 * b)

            def wide_chunks(b, m):
                if m == 0:
                    pe.wait_ge(s_wz, b + (2 - WIDE))
                pe.wait_ge(s_wt, b * 10 + (4 * m + 6 - 10 * WIDE))
                for j in range(GB):
                    for h in range(2):
                        last = mm(ps[D * h:D * h + D, m, :], wide_now[:, j, :], wide_turned[:, h, j, :],
                                  start=False, stop=False, skip_group_check=True)
                last.then_inc(s_wu, 2)

            def narrow_block(b, slot, load, n, z_before, pairs=()):
                first = isinstance(b, int) and b == 0
                for s in range(10):
                    if s % 2 == 0:
                        pe.wait_ge(s_piece[s // 2], load * 16 + 16)
                    if not (first and s == 0):
                        pe.wait_ge(s_ta, b * 10 + s)
                    turn_quad(s, 0)
                    if not (first and s == 0):
                        pe.wait_ge(s_tv, b * 10 + s)
                    if s == 0:
                        z_rows(n - 1, z_before)
                    else:
                        turn_quad(s, 1)
                    z_products(s, 0)
                    if s == 0:
                        pe.wait_ge(s_z, n)
                        turn_quad(s, 1)
                    if not first:
                        done = h_products(1 - slot, 1 - slot, s, isinstance(b, int) and b == 1, False)
                        if s == 9:
                            done.then_inc(s_p2, 1)
                    if s in pairs:
                        wide_chunks(b - slot, pairs[s])

            pe.wait_ge(s_dve, setup_at["dve"])
            for b in range(WIDE):
                wide_block(b)
                narrow_block(b, b % 2, 3 * b + 2, 2 * b + 1, wide_zT)
            with pe.Fori(WIDE, NB - 1, 2) as b:
                for i in range(2):
                    narrow_block(b + i, i, b + (2 * WIDE + i), b + (WIDE + i), zT, ({3: 0, 7: 1}, {1: 2, 5: 3, 9: 4})[i])
            pe.wait_ge(s_ta, 10 * NB)
            pe.wait_ge(s_tv, 10 * NB)
            z_rows(NB + WIDE - 1, zT)
            pe.wait_ge(s_z, NB + WIDE)
            for s in range(10):
                done = h_products((NB - 1) % 2, (NB - 1) % 2, s, False, True)
                if s % 2 == 1:
                    done.then_inc(s_p2, 1)

            for kind, _, c in MIDDLE:
                if kind == "hrows":
                    pe.wait_ge(s_act2, c + 1)
                    if c >= 2:
                        pe.wait_ge(s_dve2, mid_at["dve", "norm1", "d", c - 2])
                    for i in range(GB):
                        last = mm(ps[:, 6 + c % 2, i * P:(i + 1) * P], hT[:, c * BLK + i * P:c * BLK + (i + 1) * P],
                                  centre[:, :], start=True, stop=True)
                    last.then_inc(s_pe2, 1)
                elif kind == "weights":
                    pe.wait_ge(s_dw, GRU_IN)
                    for l in range(2):
                        ih, hh, o = raw[:, 2 * l], raw[:, 2 * l + 1], l * 2 * P
                        mm(ps[0:D, 5, o:o + P], ih[:, 0, :], ident[:, :], start=True, stop=True)
                        mm(ps[D:P, 5, o:o + P], hh[:, 0, :], ident[:, :], start=True, stop=True)
                        mm(ps[0:D, 5, o + P + D:o + 2 * P], ih[0:D, 1, :], ident[0:D, 0:D], start=True, stop=True)
                        last = mm(ps[D:P, 5, o + P:o + P + D], hh[0:D, 1, :], ident[0:D, 0:D], start=True, stop=True)
                    last.then_inc(s_pe2, 1)
                elif kind == "turn":
                    pe.wait_ge(s_dve2, mid_at["dve", "norm2", "d", c])
                    if c >= 2:
                        pe.wait_ge(s_act2, mid_at["act", "keep", "", c - 2])
                    else:
                        pe.wait_ge(s_act2, PAIRS)
                        pe.wait_ge(s_dve2, mid_at["dve", "keep_weights", "", 0])
                    for i in range(4):
                        last = nc.tensor.transpose(ps[:, 4 + c % 2, i * P:(i + 1) * P],
                                                   scratch[1][:, c, i * P:(i + 1) * P], ident[:])
                    last.then_inc(s_pe2, 1)
                elif kind == "y":
                    pe.wait_ge(s_act2, mid_at["act", "keep", "", c])
                    if c >= 1:
                        pe.wait_ge(s_dve2, mid_at["dve", "keep_y", "", c - 1])
                    for j in range(GB):
                        last = mm(ps[:, 3, j * P:(j + 1) * P], work[:, c % 2, j * P:(j + 1) * P], w_11[:],
                                  start=True, stop=True)
                    last.then_inc(s_pe2, 1)

            for step in steps:
                if step[0] in ("chunk", "cached"):
                    if step[0] == "chunk":
                        _, n, t, R, k, start = step
                        pe.wait_ge(s_turn, n + 1)
                    else:
                        _, t, R = step
                        k, start = NK, t >= NR and R == NR - 1
                    if t == 0:
                        pe.wait_ge(s_dve2, mid_at["dve", "keep_y", "", k % PAIRS])
                    elif t >= NR:
                        pe.wait_ge(s_y, k + 1)
                    if start and t >= 2:
                        pe.wait_ge(s_m, t - 1)
                    ys = y1 if t < NR else y2
                    second = t < NR and k < R and step[0] == "chunk"
                    if second:
                        pe.wait_ge(s_y, k + 1)
                        if k == 0 and R >= 3:
                            pe.wait_ge(s_m2k, R - 2)
                    ends = last_of[t] == step
                    for j in range(GB):
                        moving = (turned[:, n % NTURN, j, :] if step[0] == "chunk"
                                  else at[:, j, R * BLK:(R + 1) * BLK])
                        h = j % 2
                        last = mm(ps[D * h:D * h + D, t % 2, :], ys[:, GB * k + j, :], moving,
                                  start=start and j < 2, stop=ends and j >= 2, skip_group_check=True)
                    if ends:
                        last.then_inc(s_m1, 1)
                    if second:
                        for j in range(GB):
                            h = j % 2
                            last = mm(ps[D * h:D * h + D, 2 + R % 2, :], y2[:, GB * k + j, :],
                                      turned[:, n % NTURN, j, :], start=k == 0 and j < 2,
                                      stop=k == R - 1 and j >= 2, skip_group_check=True)
                    if step[0] == "chunk":
                        last.then_inc(s_used, 1)
                elif step[0] == "gates":
                    t = step[1]
                    l, R = t // NR, block_of(t)
                    pe.wait_ge(s_m, t + 1)
                    if t >= 1:
                        pe.wait_ge(s_u, t)
                    mm(ps[:, 4, :], w_rz[:, l, :], hs[:, R * BLK:(R + 1) * BLK], start=True, stop=True)
                    mm(ps[:, 5, :], w_n[:, l, :], hs[:, R * BLK:(R + 1) * BLK], start=True, stop=True
                       ).then_inc(s_g, 1)
                elif step[0] == "rows":
                    t = step[1]
                    R = block_of(t)
                    pe.wait_ge(s_h, t + 1)
                    if t >= 1:
                        pe.wait_ge(s_y, t)
                    for j in range(GB):
                        if t < NR:
                            last = mm(ps[:, 6, j * D:(j + 1) * D], work[D:P, 0, j * P:(j + 1) * P], w_2[D:P, :],
                                      start=True, stop=True)
                        else:
                            last = nc.tensor.transpose(ps[:, 6, j * D:(j + 1) * D],
                                                       hs[D:P, R * BLK + j * P:R * BLK + (j + 1) * P],
                                                       ident[D:P, D:P])
                    last.then_inc(s_r, 1)


_INS = ["x", "adj", "L0_gnn_W_u", "L0_gnn_diag_u", "L0_gnn_par_u", "L0_gnn_W_i", "L0_gnn_diag_i", "L0_gnn_par_i",
        "L0_gnn_ln_gamma", "L0_gnn_ln_beta", "L1_gnn_W1", "L1_gnn_wih1", "L1_gnn_whh1", "L1_gnn_bih1", "L1_gnn_bhh1",
        "L1_gnn_W2", "L1_gnn_wih2", "L1_gnn_whh2", "L1_gnn_bih2", "L1_gnn_bhh2"]
_OUTS = [((5120, 64), "float32")]


def kernel(**inputs):
    import numpy as _np
    import concourse.bacc as _bacc
    from concourse import mybir as _mybir
    from concourse.bass_utils import run_bass_kernel_spmd as _run

    nc = _bacc.Bacc("TRN2", target_bir_lowering=False, num_devices=1)
    arrays, args = {}, []
    for name in _INS:
        a = _np.ascontiguousarray(inputs[name])
        arrays[f"in_{name}_dram"] = a
        args.append(nc.dram_tensor(f"in_{name}_dram", a.shape, _mybir.dt.from_np(a.dtype), kind="ExternalInput").ap())
    for i, (shape, dtype) in enumerate(_OUTS):
        dt = _mybir.dt.from_np(_np.dtype(dtype))
        args.append(nc.dram_tensor(f"out_{i}_dram", shape, dt, kind="ExternalOutput").ap())
    bass_two_layer_gnn(nc, *args)
    r = _run(nc, [arrays], core_ids=[0])
    return r.results[0]["out_0_dram"]
```

```python
from contextlib import ExitStack

import concourse.bass as bass
from concourse import mybir

F32 = mybir.dt.float32
ALU = mybir.AluOpType
ACT = mybir.ActivationFunctionType
AX = mybir.AxisListType

P = 128
D = 64
N = 5120
G = N // P
CACHED = 4
BLK = 512
GB = BLK // P
NR = N // BLK
NK = (N - CACHED * P) // BLK
LN_EPS = 1e-5
USER_GROUPS = 16
PAIRS = 5
NSTAGE = 4
NTURN = 3
SB = 2 * P
NSB = N // SB
WIDE = 4
NB = NSB - 2 * WIDE
BUFFERS = 7
QUARTERS = ((0, 1), (2,), (3,), ())
PG = 8
NP = G // PG
CHUNK = GB * BLK


SWEEP3 = [0, 9, 1, 8, 2, 7, 3, 6, 4, 5]
LAG = ({"sum": 2, "gates": 2, "state": 4, "rows": 6},
       {"sum": 1, "gates": 5, "state": 5, "rows": 7})


def block_of(t):
    return t if t < NR else SWEEP3[t - NR]


def plan_sweeps():
    steps, chunks, late = [], [], []
    done = 0
    for t in range(2 * NR):
        R = block_of(t)
        if t == 0:
            items = [0, 5, 1, 6, 2, 7, 3, 8, 4, "cached"]
        elif t < NR:
            items = [k for k in range(NK) if k != R - 1] + ["cached", R - 1]
        else:
            items = list(range(R, NK)) + ["cached"]
        if t >= 2:
            late.sort(key=lambda entry: entry[0])
            while any(step == ("sum", t - 2) for _, _, step in late):
                steps.append(late.pop(0)[2])
        for i, item in enumerate(items):
            if item == "cached":
                steps.append(("cached", t, R))
                done += 2
            else:
                steps.append(("chunk", len(chunks), t, R, item, i == 0))
                chunks.append((R, item))
                done += 4 if t < NR and item < R else 2
            late.sort(key=lambda entry: entry[0])
            while late and late[0][0] <= done:
                steps.append(late.pop(0)[2])
        due = done
        for name in ("sum", "gates", "state", "rows"):
            due += LAG[t >= NR][name]
            before = {"gates": "state"}.get(name, name)
            due = max([due] + [d + (name == "gates") for d, u, step in late if step == (before, t - 1)])
            late.append((due, t, (name, t)))
        if 0 < t < NR:
            late.append((due, t, ("second", t)))
    late.sort(key=lambda entry: (entry[2][0] != "sum", entry[0]))
    steps += [step for _, _, step in late]
    return steps, chunks


WIDE_BUFFERS = (5, 6, 0, 4, 1, 2, 3, 5, 6, 4)


def plan_pieces():
    plan, loads, last = {}, [0] * BUFFERS, [0] * BUFFERS
    for b in range(WIDE):
        for wide, count in ((True, NR), (False, NP)):
            for n in range(count):
                buffer = WIDE_BUFFERS[n] if wide else n
                loads[buffer] += 1
                plan[b, wide, n] = (buffer, loads[buffer], last[buffer])
                last[buffer] = len(plan)
    return plan, loads


EARLY_TURNS = [("keep_y", 2), ("keep_y", 3)]
ONCE = ("diag", "coef", "weights", "keep_weights")


def skewed(stages, counts):
    order = [(kind, stage, i - lag) for i in range(PAIRS + max(s[2] for s in stages))
             for kind, stage, lag in stages if 0 <= i - lag < PAIRS and (kind not in ONCE or i == lag)]
    at = {}
    for engine, (start, per) in counts.items():
        n = start
        for step in order:
            if step[:2] in per:
                n += per[step[:2]]
                at[(engine,) + step] = n
        at[engine] = n
    return order, at


DVE_SETUP = 3

SETUP, setup_at = skewed(
    [("z", "", 7), ("coef", "", 5), ("e", "", 6), ("diag", "", 4), ("prod", "", 5), ("turn", "", 4), ("keep", "", 4),
     ("norm", "d", 3), ("norm", "c", 2), ("norm", "b", 1), ("norm", "a", 0)],
    {"dve": (DVE_SETUP, {("norm", "a"): 3, ("norm", "c"): 1, ("norm", "d"): 2, ("coef", ""): 2, ("e", ""): 2}),
     "act": (0, {("norm", "b"): 1, ("norm", "c"): 1, ("norm", "d"): 1, ("keep", ""): 1}),
     "pe": (0, {("diag", ""): 1, ("turn", ""): 1, ("prod", ""): 1})})
MIDDLE, mid_at = skewed(
    [("keep_y", "", 9), ("turn", "", 8), ("keep", "", 8), ("y", "", 8), ("norm2", "d", 7), ("norm2", "c", 6),
     ("norm2", "b", 5), ("norm2", "a", 4), ("residual", "", 3), ("norm2", "s", 4), ("norm1", "d", 2),
     ("norm1", "c", 1), ("hrows", "", 0), ("norm1", "b", 0), ("weights", "", 1), ("keep_weights", "", 1),
     ("keep_h", "", 8)],
    {"dve": (0, {("keep_weights", ""): 1, ("norm1", "c"): 1, ("norm1", "d"): 2, ("norm2", "a"): 2, ("norm2", "c"): 1,
                 ("norm2", "d"): 2, ("keep_y", ""): 1}),
     "act": (PAIRS, {("norm1", "b"): 1, ("norm1", "c"): 1, ("norm2", "b"): 1, ("norm2", "c"): 1,
                     ("keep", ""): 2, ("keep_h", ""): 2}),
     "pool": (3 * PAIRS, {("residual", ""): 2, ("norm2", "s"): 1}),
     "pe": (0, {("hrows", ""): 1, ("weights", ""): 1, ("turn", ""): 1, ("y", ""): 1})})


class Count:

    def __init__(self, sem):
        self.sem, self.n = sem, 0

    def up(self, instruction, by=1):
        self.n += by
        instruction.then_inc(self.sem, by)
        return self.n


def bass_two_layer_gnn(nc, x, adj, W_u, diag_u, par_u, W_i, diag_i, par_i, gamma, beta,
                       W1, wih1, whh1, bih1, bhh1, W2, wih2, whh2, bih2, bhh2, out):
    steps, chunks = plan_sweeps()
    pieces, piece_loads = plan_pieces()
    POOL_X = 3 * PAIRS
    with ExitStack() as ctx:
        def sb(name, shape):
            return ctx.enter_context(nc.sbuf_tensor(name, shape, F32))

        def sem(name):
            return ctx.enter_context(nc.semaphore(name))

        at = sb("at", [P, CACHED, N])
        arena = sb("arena", [P, BUFFERS * CHUNK])
        xs = sb("xs", [P, G, D])
        es = sb("es", [P, G, D])
        y1 = sb("y1", [P, G, D])
        hs = sb("hs", [P, N])
        work = sb("work", [P, 5, BLK])
        outs = sb("outs", [P, 2, GB * D])
        ident = sb("ident", [P, P])
        twice = sb("twice", [P, D])
        w_ui = sb("w_ui", [P, 2, P])
        w_11 = sb("w_11", [P, P])
        w_rz = sb("w_rz", [P, 2, P])
        w_n = sb("w_n", [P, 2, P])
        w_2 = sb("w_2", [P, D])
        gam = sb("gam", [P, D])
        bet = sb("bet", [P, D])
        b_ih = sb("b_ih", [P, 2, 2])
        b_hh = sb("b_hh", [P, 2, 2])
        b_rz = sb("b_rz", [P, 2])
        par = sb("par", [P, 2, 2])
        parp = sb("parp", [P, 2])
        dT = sb("dT", [G, P])
        coef = sb("coef", [P, G])
        eps = sb("eps", [P, 1])
        stat = sb("stat", [P, PAIRS, 4, 8])
        zT = sb("zT", [P, SB])
        zs = sb("zs", [P, 2, 2, D])
        centre = sb("centre", [P, P])

        piece = arena[:, 0:G * SB].rearrange("p (s g c) -> p s g c", s=NP, g=PG)
        wide_piece = arena[:].rearrange("p (s g c) -> p s g c", s=BUFFERS, g=GB)
        incoming = arena[:, 0:NSTAGE * CHUNK].rearrange("p (s f) -> p s f", s=NSTAGE)
        turned = arena[:, NSTAGE * CHUNK:].rearrange("p (s j i) -> p s j i", s=NTURN, j=GB)
        wide_in = arena[:, NP * CHUNK:].rearrange("p (s f) -> p s f", s=2)
        wide_turned = hs[:, 0:2 * CHUNK].rearrange("p (s j i) -> p s j i", s=2, j=GB)
        wide_zT = work[:, 0, :]
        wide_z = y1[:, 0:16, :].rearrange("p (k j) d -> p k j d", k=WIDE)
        wide_now = y1[:, 16:20, :]
        raw = y1[:, 32:40, :].rearrange("p (w h) d -> p w h d", w=4)
        h0T = y1[:, 0:16, :].rearrange("p (s g) d -> p s (g d)", s=2)
        hT = es[:].rearrange("p g d -> p (g d)")
        y2 = es
        scratch = hs[:, :].rearrange("p (s f) -> p s f", s=10)

        ps = ctx.enter_context(nc.psum_tensor("ps", [P, 8, BLK], F32))
        Z_BANK, TP_BANK = 5, 6

        s_x = [sem(f"x_chunk_loaded_{c}") for c in range(PAIRS)]
        s_w = sem("weights_loaded")
        s_idg = sem("identity_on_pool")
        s_id = sem("identity_ready")
        s_dve = sem("dve_steps")
        s_dve2 = sem("dve_mid_steps")
        s_act = sem("act_steps")
        s_act2 = sem("act_mid_steps")
        s_pe = sem("pe_setup_steps")
        s_pe2 = sem("pe_mid_steps")
        s_pool = sem("pool_steps")
        s_dw = sem("gru_weights_loaded")
        s_piece = [sem(f"piece_loaded_{i}") for i in range(BUFFERS)]
        s_pu = sem("pieces_used")
        s_tp = sem("transposes_done")
        s_ta = sem("transposes_kept_by_act")
        s_tv = sem("transposes_kept_by_dve")
        s_zc = sem("z_transposed_copied")
        s_zn = sem("z_rows_done")
        s_z = sem("z_ready")
        s_wl = [sem(f"wide_chunk_loaded_{i}") for i in range(2)]
        s_wt = sem("wide_chunks_transposed")
        s_wu = sem("wide_chunks_used")
        s_wz = sem("wide_z_copied")
        s_p2 = sem("block_product_done")
        s_stage = [sem(f"chunk_loaded_{i}") for i in range(NSTAGE)]
        s_turn = sem("chunk_transposed")
        s_used = sem("chunk_used")
        s_m1 = sem("product_done")
        s_mt = sem("upper_half_moved")
        s_m = sem("product_kept")
        s_g = sem("gates_done")
        s_rz = sem("sigmoid_done")
        s_u = sem("tanh_input_ready")
        s_n = sem("tanh_done")
        s_hv = sem("new_state_ready")
        s_h = sem("new_state_kept")
        s_r = sem("rows_done")
        s_y = sem("rows_kept")
        s_m2t = sem("second_upper_half_moved")
        s_m2k = sem("second_product_kept")
        s_gd = sem("gate_steps")
        s_out = [sem(f"stored_{i}") for i in range(2)]

        weight_loads = [
            (dT[0:USER_GROUPS, :], diag_u.rearrange("(g p) -> g p", p=P)),
            (dT[USER_GROUPS:G, :], diag_i.rearrange("(g p) -> g p", p=P)),
            (par[:, 0, :], par_u.partition_broadcast(P)),
            (par[:, 1, :], par_i.partition_broadcast(P)),
            (w_ui[0:D, 0, 0:D], W_u), (w_ui[D:P, 0, D:P], W_i),
            (w_ui[0:D, 1, 0:D], W_i), (w_ui[D:P, 1, D:P], W_i),
            (gam[:], gamma.partition_broadcast(P)), (bet[:], beta.partition_broadcast(P)),
        ]
        gru_loads = [(w_11[0:D, 0:D], W1), (w_11[D:P, D:P], W1), (w_2[D:P, :], W2)]
        for w, m in enumerate((wih1, whh1, wih2, whh2)):
            gru_loads += [(raw[:, w, 0, :], m[0:P, :]), (raw[0:D, w, 1, :], m[P:3 * D, :])]
        for l, (bi, bh) in enumerate(((bih1, bhh1), (bih2, bhh2))):
            gru_loads += [
                (b_ih[:, l, 0:1], bi[0:P].rearrange("(p o) -> p o", o=1)),
                (b_hh[:, l, 0:1], bh[0:P].rearrange("(p o) -> p o", o=1)),
                (b_ih[D:P, l, 1:2], bi[P:3 * D].rearrange("(p o) -> p o", o=1)),
                (b_hh[0:D, l, 1:2], bh[P:3 * D].rearrange("(p o) -> p o", o=1)),
            ]
        WEIGHTS_IN = 16 * len(weight_loads)
        GRU_IN = 16 * len(gru_loads)

        def pair(buf, c):
            return buf[:].rearrange("p (h g) d -> p h g d", h=2)[:, :, 4 * c:4 * c + 4, :]

        def mixed(ap):
            return ap.rearrange("p (g h d) -> p h g d", h=2, g=4)

        def spread(col):
            return col.rearrange("p (h g o) -> p h g o", h=2, o=1).broadcast_to([P, 2, 4, D])

        def rows_of(row):
            return row.rearrange("p (g d) -> p g d", g=1).broadcast_to([P, 8, D])

        def quarters(ap):
            return ap.rearrange("p (q j b) -> p q j b", q=4, b=32)

        def by_groups(ap):
            return ap.rearrange("p (j q b) -> p q j b", q=4, b=32)

        def in_group_order(R, ap):
            return quarters(ap) if R == NK else by_groups(ap)

        last_of = {s[2 if s[0] == "chunk" else 1]: s for s in steps if s[0] in ("chunk", "cached")}

        block = ctx.enter_context(nc.Block())

        @block.sync
        def _(sp):
            for c in range(PAIRS):
                for h in range(2):
                    g0 = 20 * h + 4 * c
                    sp.dma_start(xs[:, g0:g0 + 4, :], x[g0 * P:(g0 + 4) * P, :].rearrange("(g p) d -> p g d", p=P)
                                 ).then_inc(s_x[c], 16)
                if c == 2:
                    sp.wait_ge(s_dve, DVE_SETUP)
                    for dst, src in weight_loads:
                        sp.dma_start(dst, src).then_inc(s_w, 16)

            def load_piece(i, column):
                sp.dma_start(piece[:, i], adj[PG * P * i:PG * P * (i + 1), bass.ds(column, SB)].rearrange(
                    "(g p) c -> p g c", p=P)).then_inc(s_piece[i], 16)

            def load_wide_chunks(m, column):
                for h in range(2):
                    rows = adj[(m + 5 * h) * BLK:(m + 5 * h + 1) * BLK, :].rearrange("(i a) c -> a i c", a=32)
                    for q in range(4):
                        sp.dma_start(wide_in[32 * q:32 * q + 32, h].rearrange("p (i c) -> p i c", c=P),
                                     rows[:, :, bass.ds(column + q * P, P)]).then_inc(s_wl[h], 16)

            for (b, wide, n), (buffer, _, used) in sorted(pieces.items(), key=lambda piece: piece[1][2]):
                if used:
                    sp.wait_ge(s_pu, used)
                if wide:
                    row_block = n // 2 + 5 * (n % 2) if b == 0 else n
                    sp.dma_start(wide_piece[:, buffer], adj[row_block * BLK:(row_block + 1) * BLK,
                                                            b * BLK:(b + 1) * BLK]
                                 .rearrange("(g p) c -> p g c", p=P)).then_inc(s_piece[buffer], 16)
                else:
                    load_piece(n, WIDE * BLK + b * SB)
            with sp.Fori(WIDE, NB - 1, 2) as b:
                for i in range(2 * NP):
                    sp.wait_ge(s_pu, b * NP + (2 * WIDE * NP + i + 1 - NP))
                    load_piece(i % NP, b * SB + (2 * WIDE + i // NP) * SB)
                    if i in (2, 4, 6, 8, 9):
                        m = (i - 1) // 2
                        sp.wait_ge(s_wt, b * 10 + (4 * m + 2 - 10 * WIDE))
                        load_wide_chunks(m, b * SB - WIDE * SB)

            sp.wait_ge(s_pu, NP * NSB)
            for n, (R, k) in enumerate(chunks):
                slot = n % NSTAGE
                if n >= NSTAGE:
                    sp.wait_ge(s_turn, n - NSTAGE + 1)
                rows = adj[R * BLK:(R + 1) * BLK, :].rearrange("(i a) c -> a i c", a=32)
                for q in range(4):
                    sp.dma_start(incoming[32 * q:32 * q + 32, slot].rearrange("p (i c) -> p i c", c=P),
                                 rows[:, :, k * BLK + q * P:k * BLK + (q + 1) * P]).then_inc(s_stage[slot], 16)

        @block.gpsimd
        def _(pool):
            own = Count(s_idg)
            n = own.up(nc.gpsimd.memset(ident[:], 0.0))
            pool.wait_ge(s_idg, n)
            n = own.up(nc.gpsimd.affine_select(out=ident[:], in_=ident[:], compare_op=ALU.not_equal, fill=1.0, base=0,
                                               pattern=[[-1, P]], channel_multiplier=1))
            pool.wait_ge(s_dve, DVE_SETUP)
            pool.wait_ge(s_idg, n)
            nc.gpsimd.tensor_tensor(twice[:], ident[:, 0:D], ident[:, D:P], ALU.add)
            nc.gpsimd.tensor_tensor(centre[:], centre[:], ident[:], ALU.add).then_inc(s_id, 1)
            pool.wait_ge(s_w, WEIGHTS_IN)
            done = Count(s_pool)
            for c in range(PAIRS):
                pool.wait_ge(s_act, setup_at["act", "norm", "d", c])
                xv = pair(xs, c)
                n = done.up(nc.gpsimd.tensor_tensor(xv, xv, mixed(scratch[:, 5 + c, :]), ALU.add))
                pool.wait_ge(s_pool, n)
                for h in range(2):
                    v = xs[:, 20 * h + 4 * c:20 * h + 4 * c + 4, :]
                    done.up(nc.gpsimd.tensor_tensor(
                        v, v, bet[:].rearrange("p (g d) -> p g d", g=1).broadcast_to([P, 4, D]), ALU.add))

            pool.wait_ge(s_z, 2 * WIDE - 1)
            nc.gpsimd.tensor_copy(wide_now[:].rearrange("p g d -> p (g d)"),
                                  y1[:, 0:GB, :].rearrange("p g d -> p (g d)")).then_inc(s_wz, 2)
            with pool.Fori(1, WIDE) as k:
                pool.wait_ge(s_wu, k * 10 + 2)
                nc.gpsimd.tensor_copy(wide_now[:].rearrange("p g d -> p (g d)"),
                                      y1[:, 0:16, :].rearrange("p g d -> p (g d)")[:, bass.ds(k * GB * D, GB * D)]
                                      ).then_inc(s_wz, 2)

            sc = scratch
            for kind, stage, c in MIDDLE:
                if kind == "residual":
                    pool.wait_ge(s_dve2, mid_at["dve", "norm1", "d", c])
                    v = sc[:, c, :].rearrange("p (g d) -> p g d", d=D)
                    n = done.up(nc.gpsimd.tensor_tensor(v, v, rows_of(gam[:]), ALU.mult))
                    pool.wait_ge(s_pool, n)
                    done.up(nc.gpsimd.tensor_tensor(pair(xs, c), mixed(sc[:, c, :]), pair(xs, c), ALU.add))
                elif kind == "norm2" and stage == "s":
                    pool.wait_ge(s_dve2, mid_at["dve", "norm2", "a", c])
                    pool.wait_ge(s_pool, mid_at["pool", "residual", "", c])
                    done.up(nc.gpsimd.tensor_tensor(mixed(sc[:, c, :]), pair(xs, c), spread(stat[:, c, 0, :]),
                                                    ALU.add))

            for step in steps:
                if step[0] == "state" and step[1] < 2 * NR - 1:
                    t = step[1]
                    R = block_of(t)
                    pool.wait_ge(s_n, t + 1)
                    n = done.up(nc.gpsimd.tensor_tensor(work[D:P, 2, :], hs[D:P, R * BLK:(R + 1) * BLK],
                                                        work[D:P, 3, :], ALU.subtract))
                    pool.wait_ge(s_pool, n)
                    n = done.up(nc.gpsimd.tensor_tensor(work[D:P, 2, :], work[D:P, 2, :], work[D:P, 1, :], ALU.mult))
                    pool.wait_ge(s_pool, n)
                    nc.gpsimd.tensor_tensor(work[D:P, 2, :], work[D:P, 2, :], work[D:P, 3, :], ALU.add
                                            ).then_inc(s_hv, 1)

        @block.scalar
        def _(act):
            def squares(c, s_a):
                nc.scalar.activation(scratch[:, 5 + c, :], scratch[:, c, :], ACT.Square).then_inc(s_a, 1)

            def deviation(c, s_a):
                nc.scalar.activation(stat[:, c, 2, :], stat[:, c, 1, :], ACT.Sqrt, bias=eps[:], scale=1.0 / D
                                     ).then_inc(s_a, 1)

            for kind, stage, c in SETUP:
                if kind == "norm" and stage == "b":
                    act.wait_ge(s_dve, setup_at["dve", "norm", "a", c])
                    squares(c, s_act)
                elif kind == "norm" and stage == "c":
                    act.wait_ge(s_dve, setup_at["dve", "norm", "c", c])
                    deviation(c, s_act)
                elif kind == "norm" and stage == "d":
                    act.wait_ge(s_dve, setup_at["dve", "norm", "d", c])
                    nc.scalar.activation(scratch[:, 5 + c, :], scratch[:, c, :], ACT.Relu).then_inc(s_act, 1)
                elif kind == "keep":
                    act.wait_ge(s_pe, setup_at["pe", "turn", "", c])
                    if c >= 2:
                        act.wait_ge(s_pe, setup_at["pe", "prod", "", c - 2])
                    nc.scalar.activation(h0T[:, c % 2, :], ps[:, c % 2, :], ACT.Copy).then_inc(s_act, 1)

            act.wait_ge(s_dve, DVE_SETUP)
            for dst, src in gru_loads:
                act.dma_start(dst, src).then_inc(s_dw, 16)

            def keep_z(n, rows):
                act.wait_ge(s_zn, n + 1)
                nc.scalar.activation(rows.rearrange("p j d -> p (j d)"),
                                     ps[:, TP_BANK + 1, 0:rows.shape[1] * D], ACT.Copy).then_inc(s_z, 1)

            def keep_transposes(b, slot, z_before=None):
                for s in range(10):
                    act.wait_ge(s_tp, b * 20 + (2 * s + 1))
                    if s == 0 and (not isinstance(b, int) or b >= 2):
                        act.wait_ge(s_p2, b - 1)
                    nc.scalar.activation(at[:, 2 * slot, s * BLK:(s + 1) * BLK], ps[:, TP_BANK, :], ACT.Copy
                                         ).then_inc(s_ta, 1)
                    if s == 0:
                        keep_z(*z_before)

            for b in range(WIDE):
                if b:
                    keep_z(2 * b - 1, zs[:, (b - 1) % 2])
                keep_transposes(b, b % 2, (2 * b, wide_z[:, b]))
            with act.Fori(WIDE, NB - 1, 2) as b:
                for i in range(2):
                    keep_transposes(b + i, i, (b + (WIDE + i - 1), zs[:, 1 - i]))
            keep_z(NB + WIDE - 1, zs[:, (NB - 1) % 2])

            for c in range(PAIRS):
                act.wait_ge(s_p2, NB + c)
                nc.scalar.activation(hT[:, c * BLK:(c + 1) * BLK], ps[:, c, :], ACT.Copy).then_inc(s_act2, 1)
            for kind, stage, c in MIDDLE:
                if kind == "norm1" and stage == "b":
                    act.wait_ge(s_pe2, mid_at["pe", "hrows", "", c])
                    nc.scalar.activation(scratch[:, 5 + c, :], ps[:, 6 + c % 2, :], ACT.Square
                                         ).then_inc(s_act2, 1)
                elif kind == "norm2" and stage == "b":
                    act.wait_ge(s_pool, mid_at["pool", "norm2", "s", c])
                    squares(c, s_act2)
                elif kind in ("norm1", "norm2") and stage == "c":
                    act.wait_ge(s_dve2, mid_at["dve", kind, "c", c])
                    deviation(c, s_act2)
                elif kind == "keep":
                    act.wait_ge(s_pe2, mid_at["pe", "turn", "", c])
                    if c >= 2:
                        act.wait_ge(s_pe2, mid_at["pe", "y", "", c - 2])
                    for h in range(2):
                        half = slice(D * h, D * h + D)
                        nc.scalar.activation(in_group_order(c + 5 * h, work[half, c % 2, :]),
                                             quarters(ps[half, 4 + c % 2, :]), ACT.Relu).then_inc(s_act2, 1)
                elif kind == "keep_h":
                    for h in range(2):
                        nc.scalar.activation(hs[D:P, (c + 5 * h) * BLK:(c + 5 * h + 1) * BLK],
                                             ps[D * h:D * h + D, 4 + c % 2, :], ACT.Relu).then_inc(s_act2, 1)

            for step in steps:
                if step[0] == "sum":
                    t = step[1]
                    act.wait_ge(s_m1, t + 1)
                    if t > 0:
                        act.wait_ge(s_m, t)
                    nc.scalar.activation(work[0:D, 0, :], ps[D:P, t % 2, :], ACT.Copy).then_inc(s_mt, 1)
                elif step[0] == "gates":
                    t = step[1]
                    act.wait_ge(s_g, t + 1)
                    if t > 0:
                        act.wait_ge(s_hv, t)
                    nc.scalar.activation(work[:, 1, :], ps[:, 4, :], ACT.Sigmoid, bias=b_rz[:, t // NR:t // NR + 1]
                                         ).then_inc(s_rz, 1)
                elif step[0] == "state":
                    t = step[1]
                    l, R = t // NR, block_of(t)
                    cols = slice(R * BLK, (R + 1) * BLK)
                    act.wait_ge(s_u, t + 1)
                    nc.scalar.activation(work[D:P, 3, :], work[D:P, 2, :], ACT.Tanh, bias=b_ih[D:P, l, 1:2]
                                         ).then_inc(s_n, 1)
                    act.wait_ge(s_hv, t + 1)
                    if t < NR:
                        nc.scalar.activation(hs[D:P, cols], work[D:P, 2, :], ACT.Relu)
                        nc.scalar.activation(in_group_order(R, work[D:P, 0, :]), quarters(work[D:P, 2, :]), ACT.Relu
                                             ).then_inc(s_h, 1)
                    else:
                        nc.scalar.activation(hs[D:P, cols], work[D:P, 2, :], ACT.Relu).then_inc(s_h, 1)
                elif step[0] == "rows":
                    t = step[1]
                    R = block_of(t)
                    if t < NR:
                        act.wait_ge(s_r, t + 1)
                        nc.scalar.activation(y2[:, GB * R:GB * R + GB, :].rearrange("p g d -> p (g d)"),
                                             ps[:, 6, 0:GB * D], ACT.Copy).then_inc(s_y, 1)
                    else:
                        act.wait_ge(s_y, t + 1)
                        act.dma_start(out[R * BLK:(R + 1) * BLK, :].rearrange("(g p) d -> p g d", p=P),
                                      outs[:, t % 2, :].rearrange("p (g d) -> p g d", d=D)
                                      ).then_inc(s_out[t % 2], 16)
                elif step[0] == "second":
                    R = step[1]
                    act.wait_ge(s_used, last_of[R][1] + 1)
                    if R > 1:
                        act.wait_ge(s_m2k, R - 1)
                    nc.scalar.activation(work[0:D, 4, :], ps[D:P, 2 + R % 2, :], ACT.Copy).then_inc(s_m2t, 1)
            for i in range(2):
                act.wait_ge(s_out[i], 16 * (NR // 2))

        @block.vector
        def _(dve):
            own = Count(s_dve)
            own.up(nc.vector.memset(eps[:], LN_EPS))
            nc.vector.memset(w_ui[:], 0.0).then_inc(s_wt, 2)
            nc.vector.memset(w_11[:], 0.0)
            own.up(nc.vector.memset(w_n[:], 0.0))
            for h in range(2):
                nc.vector.memset(centre[D * h:D * h + D, D * (1 - h):D * (1 - h) + D], 0.0)
                last = nc.vector.memset(centre[D * h:D * h + D, D * h:D * h + D], -1.0 / D)
            own.up(last)
            assert own.n == DVE_SETUP

            def sum_of_squares(cnt, c, sc):
                cnt.up(nc.vector.tensor_reduce(stat[:, c, 1, :], mixed(sc[:, 5 + c, :]), AX.X, ALU.add))

            def minus_mean(cnt, c, src):
                n = cnt.up(nc.vector.tensor_reduce(stat[:, c, 0, :], src, AX.X, ALU.add))
                dve.wait_ge(cnt.sem, n)
                return cnt.up(nc.vector.tensor_scalar(stat[:, c, 0, :], stat[:, c, 0, :], -1.0 / D, None, ALU.mult))

            def scaled(cnt, c, src, sc):
                n = cnt.up(nc.vector.reciprocal(stat[:, c, 3, :], stat[:, c, 2, :]))
                dve.wait_ge(cnt.sem, n)
                cnt.up(nc.vector.tensor_tensor(mixed(sc[:, c, :]), src, spread(stat[:, c, 3, :]), ALU.mult))

            for kind, stage, c in SETUP:
                if kind == "norm" and stage == "a":
                    dve.wait_ge(s_x[c], 32)
                    n = minus_mean(own, c, pair(xs, c))
                    dve.wait_ge(s_dve, n)
                    own.up(nc.vector.tensor_tensor(mixed(scratch[:, c, :]), pair(xs, c), spread(stat[:, c, 0, :]),
                                                   ALU.add))
                elif kind == "norm" and stage == "c":
                    dve.wait_ge(s_act, setup_at["act", "norm", "b", c])
                    sum_of_squares(own, c, scratch)
                elif kind == "norm" and stage == "d":
                    dve.wait_ge(s_act, setup_at["act", "norm", "c", c])
                    scaled(own, c, mixed(scratch[:, c, :]), scratch)
                elif kind == "coef":
                    dve.wait_ge(s_w, WEIGHTS_IN)
                    n = own.up(nc.vector.tensor_tensor(parp[:], par[:, :, 0], par[:, :, 1], ALU.mult))
                    dve.wait_ge(s_dve, n)
                    dve.wait_ge(s_pe, setup_at["pe", "diag", "", 0])
                    nc.vector.tensor_scalar(coef[:, 0:USER_GROUPS], ps[:, 7, 0:USER_GROUPS], parp[:, 0:1], None,
                                            ALU.mult)
                    n = own.up(nc.vector.tensor_scalar(coef[:, USER_GROUPS:G], ps[:, 7, USER_GROUPS:G], parp[:, 1:2],
                                                       None, ALU.mult))
                    dve.wait_ge(s_dve, n)
                elif kind == "e":
                    dve.wait_ge(s_pe, setup_at["pe", "prod", "", c])
                    scale = coef[:].rearrange("p (h g o) -> p h g o", h=2, o=1)[:, :, 4 * c:4 * c + 4, :]
                    last = nc.vector.tensor_tensor(pair(es, c), mixed(ps[:, 4, :]), scale.broadcast_to([P, 2, 4, D]),
                                                   ALU.mult)
                    n = own.up(last)
                    dve.wait_ge(s_dve, n)
                    own.up(nc.vector.tensor_tensor(pair(es, c), pair(es, c), mixed(scratch[:, 5 + c, :]), ALU.add))
            assert own.n == setup_at["dve"]

            def keep_transposes(b, slot, quarters_at=None):
                for s in range(10):
                    dve.wait_ge(s_tp, b * 20 + (2 * s + 2))
                    if s == 0 and (not isinstance(b, int) or b >= 2):
                        dve.wait_ge(s_p2, b - 1)
                    nc.vector.tensor_copy(at[:, 2 * slot + 1, s * BLK:(s + 1) * BLK], ps[:, TP_BANK + 1, :]
                                          ).then_inc(s_tv, 1)
                    for quarter in (quarters_at or {}).get(s, ()):
                        turn_wide_quarter(b - slot, *quarter)

            def turn_wide_quarter(b, m, quarter):
                h, half = quarter // 2, quarter % 2
                if quarter == 0:
                    dve.wait_ge(s_wu, b * 5 + (2 * m + 2 - 5 * WIDE))
                if half == 0:
                    dve.wait_ge(s_wl[h], b * 160 + (64 * m + 64 - 160 * WIDE))
                nc.vector.transpose(
                    wide_turned[:, h, :, BLK // 2 * half:BLK // 2 * (half + 1)].rearrange("p j (i a) -> p i j a", a=32),
                    wide_in[:, h, CHUNK // 2 * half:CHUNK // 2 * (half + 1)].rearrange("p (i j b) -> p i j b",
                                                                                       j=GB, b=32)
                    ).then_inc(s_wt, 1)

            def keep_zT(loads):
                dve.wait_ge(s_pu, loads * NP)
                nc.vector.tensor_copy(zT[:], ps[:, Z_BANK, 0:SB]).then_inc(s_zc, 1)

            for b in range(WIDE):
                if b:
                    keep_zT(3 * b)
                dve.wait_ge(s_pu, (3 * b + 2) * NP)
                nc.vector.tensor_copy(by_groups(wide_zT), quarters(ps[:, Z_BANK, :])).then_inc(s_zc, 1)
                keep_transposes(b, b % 2)

            def wide_quarters(i):
                return {s: [((10 * i + s) // 4, q) for q in QUARTERS[(10 * i + s) % 4]] for s in range(10)}

            dve.wait_ge(s_pool, POOL_X)
            with dve.Fori(WIDE, NB - 1, 2) as b:
                for i in range(2):
                    keep_zT(b + (2 * WIDE + i))
                    keep_transposes(b + i, i, wide_quarters(i))
            keep_zT(NSB)

            def turn_chunk(n):
                slot, to = n % NSTAGE, n % NTURN
                dve.wait_ge(s_stage[slot], 64 * (n // NSTAGE + 1))
                if n >= NTURN:
                    dve.wait_ge(s_used, n - NTURN + 1)
                nc.vector.transpose(turned[:, to].rearrange("p j (i a) -> p i j a", a=32),
                                    incoming[:, slot].rearrange("p (i j b) -> p i j b", j=GB, b=32)
                                    ).then_inc(s_turn, 1)

            mid = Count(s_dve2)
            sc = scratch
            for kind, stage, c in MIDDLE:
                if kind == "keep_weights":
                    dve.wait_ge(s_pe2, mid_at["pe", "weights", "", 0])
                    nc.vector.tensor_tensor(b_rz[:], b_ih[:, :, 0], b_hh[:, :, 0], ALU.add)
                    for l in range(2):
                        nc.vector.tensor_copy(w_rz[:, l, :], ps[:, 5, l * 2 * P:l * 2 * P + P])
                        nc.vector.tensor_copy(w_n[0:D, l, D:P], ps[0:D, 5, l * 2 * P + P + D:l * 2 * P + 2 * P])
                        last = nc.vector.tensor_copy(w_n[D:P, l, 0:D], ps[D:P, 5, l * 2 * P + P:l * 2 * P + P + D])
                    mid.up(last)
                elif kind in ("norm1", "norm2") and stage == "c":
                    dve.wait_ge(s_act2, mid_at["act", kind, "b", c])
                    sum_of_squares(mid, c, sc)
                elif kind == "norm1" and stage == "d":
                    dve.wait_ge(s_act2, mid_at["act", "norm1", "c", c])
                    scaled(mid, c, ps[:, 6 + c % 2, :].rearrange("p (g h d) -> p h g d", h=2, d=D), sc)
                elif kind == "norm2" and stage == "a":
                    dve.wait_ge(s_pool, mid_at["pool", "residual", "", c])
                    minus_mean(mid, c, pair(xs, c))
                elif kind == "norm2" and stage == "d":
                    dve.wait_ge(s_act2, mid_at["act", "norm2", "c", c])
                    scaled(mid, c, mixed(sc[:, c, :]), sc)
                elif kind == "keep_y":
                    dve.wait_ge(s_pe2, mid_at["pe", "y", "", c])
                    mid.up(nc.vector.tensor_copy(pair(y1, c), mixed(ps[:, 3, :])))
                if (kind, c) in EARLY_TURNS:
                    turn_chunk(EARLY_TURNS.index((kind, c)))
            assert mid.n == mid_at["dve"]

            g = Count(s_gd)
            for step in steps:
                if step[0] == "chunk":
                    if step[1] + 2 < len(chunks):
                        turn_chunk(step[1] + 2)
                elif step[0] == "sum":
                    t = step[1]
                    R = block_of(t)
                    cols = slice(R * BLK, (R + 1) * BLK)
                    dve.wait_ge(s_mt, t + 1)
                    if t >= NR and R > 0:
                        n = g.up(nc.vector.tensor_tensor(work[0:D, 0, :], work[0:D, 0, :], hs[0:D, cols], ALU.add))
                        dve.wait_ge(s_gd, n)
                    nc.vector.tensor_tensor(hs[0:D, cols], ps[0:D, t % 2, :], work[0:D, 0, :], ALU.add
                                            ).then_inc(s_m, 1)
                elif step[0] == "gates":
                    t = step[1]
                    l = t // NR
                    dve.wait_ge(s_rz, t + 1)
                    n = g.up(nc.vector.scalar_tensor_tensor(out=work[D:P, 2, :], in0=ps[0:D, 5, :],
                                                            scalar=b_hh[0:D, l, 1:2], in1=work[0:D, 1, :],
                                                            op0=ALU.add, op1=ALU.mult))
                    dve.wait_ge(s_gd, n)
                    nc.vector.tensor_tensor(work[D:P, 2, :], ps[D:P, 5, :], work[D:P, 2, :], ALU.add
                                            ).then_inc(s_u, 1)
                elif step == ("state", 2 * NR - 1):
                    R = block_of(step[1])
                    dve.wait_ge(s_n, 2 * NR)
                    n = g.up(nc.vector.tensor_tensor(work[D:P, 2, :], hs[D:P, R * BLK:(R + 1) * BLK],
                                                     work[D:P, 3, :], ALU.subtract))
                    dve.wait_ge(s_gd, n)
                    n = g.up(nc.vector.tensor_tensor(work[D:P, 2, :], work[D:P, 2, :], work[D:P, 1, :], ALU.mult))
                    dve.wait_ge(s_gd, n)
                    nc.vector.tensor_tensor(work[D:P, 2, :], work[D:P, 2, :], work[D:P, 3, :], ALU.add
                                            ).then_inc(s_hv, 1)
                elif step[0] == "rows" and step[1] >= NR:
                    t = step[1]
                    R = block_of(t)
                    dve.wait_ge(s_r, t + 1)
                    if t >= NR + 2:
                        dve.wait_ge(s_out[t % 2], 16 * ((t - NR) // 2))
                    nc.vector.tensor_tensor(outs[:, t % 2, :], ps[:, 6, 0:GB * D],
                                            xs[:, GB * R:GB * R + GB, :].rearrange("p g d -> p (g d)"), ALU.add
                                            ).then_inc(s_y, 1)
                elif step[0] == "second":
                    R = step[1]
                    dve.wait_ge(s_m2t, R)
                    nc.vector.tensor_tensor(hs[0:D, R * BLK:(R + 1) * BLK], ps[0:D, 2 + R % 2, :], work[0:D, 4, :],
                                            ALU.add).then_inc(s_m2k, 1)

        @block.tensor
        def _(pe):
            mm = nc.tensor.matmul
            pe.wait_ge(s_id, 1)

            def wide_z_products(n, b, row_block):
                buffer, loads, _ = pieces[b, True, n]
                pe.wait_ge(s_piece[buffer], 16 * loads)
                for r in range(GB):
                    last = mm(ps[D * (r % 2):D * (r % 2) + D, Z_BANK, :], es[:, row_block * GB + r, :],
                              wide_piece[:, buffer, r, :], start=n == 0 and r < 2, stop=n == NR - 1 and r >= 2,
                              skip_group_check=True)
                last.then_inc(s_pu, 1)

            for kind, _, c in SETUP:
                if kind == "z":
                    pe.wait_ge(s_dve, setup_at["dve", "e", "", c])
                    wide_z_products(2 * c, 0, c)
                    wide_z_products(2 * c + 1, 0, c + 5)
                elif kind == "turn":
                    pe.wait_ge(s_act, setup_at["act", "norm", "d", c])
                    if c >= 2:
                        pe.wait_ge(s_act, setup_at["act", "keep", "", c - 2])
                    for i in range(4):
                        last = nc.tensor.transpose(ps[:, c % 2, i * P:(i + 1) * P],
                                                   scratch[:, 5 + c, i * P:(i + 1) * P], ident[:])
                        if c == 0 and i == 0:
                            last.then_inc(s_wu, 2)
                    last.then_inc(s_pe, 1)
                elif kind == "diag":
                    pe.wait_ge(s_w, WEIGHTS_IN)
                    mm(ps[:, 7, 0:G], dT[:, :], ident[0:G, 0:G], start=True, stop=True).then_inc(s_pe, 1)
                elif kind == "prod":
                    pe.wait_ge(s_act, setup_at["act", "keep", "", c])
                    if c:
                        pe.wait_ge(s_dve, setup_at["dve", "e", "", c - 1])
                    for i in range(GB):
                        last = mm(ps[:, 4, i * P:(i + 1) * P], h0T[:, c % 2, i * P:(i + 1) * P],
                                  w_ui[:, 0 if 4 * c + i < USER_GROUPS else 1, :], start=True, stop=True)
                    last.then_inc(s_pe, 1)

            def h_products(slot, half, s, first, last_block):
                bank, j = s // 2, s % 2
                for h in range(2):
                    done = mm(ps[D * h:D * h + D, bank, :], zs[:, half, j, :],
                              at[:, 2 * slot + j, (h * 5 + bank) * BLK:(h * 5 + bank + 1) * BLK],
                              start=first and j == 0, stop=last_block and j == 1, skip_group_check=True)
                return done

            def z_rows(n, rows_T):
                pe.wait_ge(s_zc, n + 1)
                for j in range(rows_T.shape[1] // P):
                    last = mm(ps[:, TP_BANK + 1, j * D:(j + 1) * D], rows_T[:, j * P:(j + 1) * P], twice[:],
                              start=True, stop=True, skip_group_check=True)
                last.then_inc(s_zn, 1)

            def turn_quad(s, j):
                for i in range(4):
                    g = 4 * s + i
                    last = nc.tensor.transpose(ps[:, TP_BANK + j, i * P:(i + 1) * P],
                                               piece[:, g // PG, g % PG, j * P:(j + 1) * P], ident[:])
                last.then_inc(s_tp, 1)

            def z_products(s):
                for i in range(4):
                    g = 4 * s + i
                    last = mm(ps[D * (g % 2):D * (g % 2) + D, Z_BANK, 0:SB], es[:, g, :],
                              piece[:, g // PG, g % PG, :], start=g < 2, stop=g >= G - 2, skip_group_check=True)
                if s % 2 == 1:
                    last.then_inc(s_pu, 1)

            def wide_block(b):
                pe.wait_ge(s_tv, b * 10)
                z_rows(2 * b - 1, zT)
                for n in range(NR):
                    wide_z_products(n, b, n)
                pe.wait_ge(s_z, 2 * b)

            def wide_chunks(b, m):
                if m == 0:
                    pe.wait_ge(s_wz, b + (2 - WIDE))
                pe.wait_ge(s_wt, b * 10 + (4 * m + 6 - 10 * WIDE))
                for j in range(GB):
                    for h in range(2):
                        last = mm(ps[D * h:D * h + D, m, :], wide_now[:, j, :], wide_turned[:, h, j, :],
                                  start=False, stop=False, skip_group_check=True)
                last.then_inc(s_wu, 2)

            def narrow_block(b, slot, loads, n, z_before, pairs=()):
                first = isinstance(b, int) and b == 0
                for s in range(10):
                    if s % 2 == 0:
                        pe.wait_ge(s_piece[s // 2], loads[s // 2] * 16)
                    if not (first and s == 0):
                        pe.wait_ge(s_ta, b * 10 + s)
                    turn_quad(s, 0)
                    if not (first and s == 0):
                        pe.wait_ge(s_tv, b * 10 + s)
                    if s == 0:
                        z_rows(n - 1, z_before)
                    else:
                        turn_quad(s, 1)
                    z_products(s)
                    if s == 0:
                        pe.wait_ge(s_z, n)
                        turn_quad(s, 1)
                    if not first:
                        done = h_products(1 - slot, 1 - slot, s, isinstance(b, int) and b == 1, False)
                        if s == 9:
                            done.then_inc(s_p2, 1)
                    if s in pairs:
                        wide_chunks(b - slot, pairs[s])

            for b in range(WIDE):
                if b:
                    wide_block(b)
                narrow_block(b, b % 2, [pieces[b, False, i][1] for i in range(NP)], 2 * b + 1, wide_zT)
            with pe.Fori(WIDE, NB - 1, 2) as b:
                for i in range(2):
                    narrow_block(b + i, i, [b + (piece_loads[j] + 1 + i - WIDE) for j in range(NP)], b + (WIDE + i), zT,
                                 ({3: 0, 7: 1}, {1: 2, 5: 3, 9: 4})[i])
            pe.wait_ge(s_ta, 10 * NB)
            pe.wait_ge(s_tv, 10 * NB)
            z_rows(NB + WIDE - 1, zT)
            pe.wait_ge(s_z, NB + WIDE)
            for s in range(10):
                done = h_products((NB - 1) % 2, (NB - 1) % 2, s, False, True)
                if s % 2 == 1:
                    done.then_inc(s_p2, 1)

            for kind, _, c in MIDDLE:
                if kind == "hrows":
                    pe.wait_ge(s_act2, c + 1)
                    if c >= 2:
                        pe.wait_ge(s_dve2, mid_at["dve", "norm1", "d", c - 2])
                    for i in range(GB):
                        last = mm(ps[:, 6 + c % 2, i * P:(i + 1) * P], hT[:, c * BLK + i * P:c * BLK + (i + 1) * P],
                                  centre[:, :], start=True, stop=True)
                    last.then_inc(s_pe2, 1)
                elif kind == "weights":
                    pe.wait_ge(s_dw, GRU_IN)
                    for l in range(2):
                        ih, hh, o = raw[:, 2 * l], raw[:, 2 * l + 1], l * 2 * P
                        mm(ps[0:D, 5, o:o + P], ih[:, 0, :], ident[:, :], start=True, stop=True)
                        mm(ps[D:P, 5, o:o + P], hh[:, 0, :], ident[:, :], start=True, stop=True)
                        mm(ps[0:D, 5, o + P + D:o + 2 * P], ih[0:D, 1, :], ident[0:D, 0:D], start=True, stop=True)
                        last = mm(ps[D:P, 5, o + P:o + P + D], hh[0:D, 1, :], ident[0:D, 0:D], start=True, stop=True)
                    last.then_inc(s_pe2, 1)
                elif kind == "turn":
                    pe.wait_ge(s_dve2, mid_at["dve", "norm2", "d", c])
                    if c >= 2:
                        pe.wait_ge(s_act2, mid_at["act", "keep_h", "", c - 2])
                    else:
                        pe.wait_ge(s_act2, PAIRS)
                        pe.wait_ge(s_dve2, mid_at["dve", "keep_weights", "", 0])
                    for i in range(4):
                        last = nc.tensor.transpose(ps[:, 4 + c % 2, i * P:(i + 1) * P],
                                                   scratch[:, c, i * P:(i + 1) * P], ident[:])
                    last.then_inc(s_pe2, 1)
                elif kind == "y":
                    pe.wait_ge(s_act2, mid_at["act", "keep", "", c])
                    if c >= 1:
                        pe.wait_ge(s_dve2, mid_at["dve", "keep_y", "", c - 1])
                    for j in range(GB):
                        last = mm(ps[:, 3, j * P:(j + 1) * P], work[:, c % 2, j * P:(j + 1) * P], w_11[:],
                                  start=True, stop=True)
                    last.then_inc(s_pe2, 1)

            for step in steps:
                if step[0] in ("chunk", "cached"):
                    if step[0] == "chunk":
                        _, n, t, R, k, start = step
                        pe.wait_ge(s_turn, n + 1)
                    else:
                        _, t, R = step
                        k, start = NK, t >= NR and R == NR - 1
                    if t == 0:
                        pe.wait_ge(s_dve2, mid_at["dve", "keep_y", "", k % PAIRS])
                    elif t >= NR:
                        pe.wait_ge(s_y, k + 1)
                    if start and t >= 2:
                        pe.wait_ge(s_m, t - 1)
                    ys = y1 if t < NR else y2
                    second = t < NR and k < R and step[0] == "chunk"
                    if second:
                        pe.wait_ge(s_y, k + 1)
                        if k == 0 and R >= 3:
                            pe.wait_ge(s_m2k, R - 2)
                    ends = last_of[t] == step
                    for j in range(GB):
                        moving = (turned[:, n % NTURN, j, :] if step[0] == "chunk"
                                  else at[:, j, R * BLK:(R + 1) * BLK])
                        h = j % 2
                        last = mm(ps[D * h:D * h + D, t % 2, :], ys[:, GB * k + j, :], moving,
                                  start=start and j < 2, stop=ends and j >= 2, skip_group_check=True)
                    if ends:
                        last.then_inc(s_m1, 1)
                    if second:
                        for j in range(GB):
                            h = j % 2
                            last = mm(ps[D * h:D * h + D, 2 + R % 2, :], y2[:, GB * k + j, :],
                                      turned[:, n % NTURN, j, :], start=k == 0 and j < 2,
                                      stop=k == R - 1 and j >= 2, skip_group_check=True)
                    if step[0] == "chunk":
                        last.then_inc(s_used, 1)
                elif step[0] == "gates":
                    t = step[1]
                    l, R = t // NR, block_of(t)
                    pe.wait_ge(s_m, t + 1)
                    if t >= 1:
                        pe.wait_ge(s_u, t)
                    mm(ps[:, 4, :], w_rz[:, l, :], hs[:, R * BLK:(R + 1) * BLK], start=True, stop=True)
                    mm(ps[:, 5, :], w_n[:, l, :], hs[:, R * BLK:(R + 1) * BLK], start=True, stop=True
                       ).then_inc(s_g, 1)
                elif step[0] == "rows":
                    t = step[1]
                    R = block_of(t)
                    pe.wait_ge(s_h, t + 1)
                    if t >= 1:
                        pe.wait_ge(s_y, t)
                    for j in range(GB):
                        if t < NR:
                            last = mm(ps[:, 6, j * D:(j + 1) * D], work[D:P, 0, j * P:(j + 1) * P], w_2[D:P, :],
                                      start=True, stop=True)
                        else:
                            last = nc.tensor.transpose(ps[:, 6, j * D:(j + 1) * D],
                                                       hs[D:P, R * BLK + j * P:R * BLK + (j + 1) * P],
                                                       ident[D:P, D:P])
                    last.then_inc(s_r, 1)


_INS = ["x", "adj", "L0_gnn_W_u", "L0_gnn_diag_u", "L0_gnn_par_u", "L0_gnn_W_i", "L0_gnn_diag_i", "L0_gnn_par_i",
        "L0_gnn_ln_gamma", "L0_gnn_ln_beta", "L1_gnn_W1", "L1_gnn_wih1", "L1_gnn_whh1", "L1_gnn_bih1", "L1_gnn_bhh1",
        "L1_gnn_W2", "L1_gnn_wih2", "L1_gnn_whh2", "L1_gnn_bih2", "L1_gnn_bhh2"]
_OUTS = [((5120, 64), "float32")]


def kernel(**inputs):
    import numpy as _np
    import concourse.bacc as _bacc
    from concourse import mybir as _mybir
    from concourse.bass_utils import run_bass_kernel_spmd as _run

    nc = _bacc.Bacc("TRN2", target_bir_lowering=False, num_devices=1)
    arrays, args = {}, []
    for name in _INS:
        a = _np.ascontiguousarray(inputs[name])
        arrays[f"in_{name}_dram"] = a
        args.append(nc.dram_tensor(f"in_{name}_dram", a.shape, _mybir.dt.from_np(a.dtype), kind="ExternalInput").ap())
    for i, (shape, dtype) in enumerate(_OUTS):
        dt = _mybir.dt.from_np(_np.dtype(dtype))
        args.append(nc.dram_tensor(f"out_{i}_dram", shape, dt, kind="ExternalOutput").ap())
    bass_two_layer_gnn(nc, *args)
    r = _run(nc, [arrays], core_ids=[0])
    return r.results[0]["out_0_dram"]
```
